# Optimizing a Trainium2 kernel written in Bass

```python
import numpy as np
import jax
import jax.numpy as jnp

def _softmax(x, axis=-1):
    return jax.nn.softmax(x, axis=axis)

def _gelu(x):
    return jax.nn.gelu(x, approximate=True)

def _silu(x):
    return jax.nn.silu(x)

def _sigmoid(x):
    return jax.nn.sigmoid(x)

def _layernorm(x, axis=-1, eps=1e-05):
    m = jnp.mean(x, axis=axis, keepdims=True)
    v = jnp.var(x, axis=axis, keepdims=True)
    return (x - m) / jnp.sqrt(v + eps)

def _scatter_add(tgt, idx, src, axis=0):
    return tgt.at[idx].add(src)

def _segment_sum(src, seg, n):
    return jax.ops.segment_sum(src, seg, n)
kernel_name = 'mk_vit_tower_d2_tok_img256_r4_cf2a62'

def setup_inputs(seed: int=0):
    np.random.seed(seed)
    _w = jnp.asarray

    def _rec_inputs():
        import jax
        import jax.numpy as jnp
        _rk = jax.random.key(seed)
        x = -0.000125008 + 0.999885 * jax.random.normal(jax.random.fold_in(_rk, 1), (4, 64, 64, 64), jnp.float32)
        return x
    x = _rec_inputs()

    def _L0_tok_setup():
        import jax, jax.numpy as jnp
        import numpy as np
        DIM = 64
        NH = 8
        WH, WW = (8, 8)

        def _rope_axis(x, axis):
            half = x.shape[-1]
            inv_freq = 1.0 / 10000.0 ** (jnp.arange(0, half, 2, dtype=jnp.float32) / half)
            pos = jnp.arange(x.shape[axis], dtype=jnp.float32)
            ang = pos[:, None] * inv_freq
            cos, sin = (jnp.cos(ang), jnp.sin(ang))
            shape = [1, 1, 1, ang.shape[-1]]
            shape[axis] = ang.shape[0]
            cos = cos.reshape(shape).astype(x.dtype)
            sin = sin.reshape(shape).astype(x.dtype)
            x1, x2 = (x[..., 0::2], x[..., 1::2])
            r1 = x1 * cos - x2 * sin
            r2 = x1 * sin + x2 * cos
            return jnp.stack([r1, r2], axis=-1).reshape(x.shape)

        def _rope2(x):
            half = x.shape[-1] // 2
            return jnp.concatenate([_rope_axis(x[..., :half], 1), _rope_axis(x[..., half:], 2)], axis=-1)
        key = jax.random.key(seed)
        ks = jax.random.split(key, 5)
        B, H, W, C = (32, 64, 64, DIM)
        s = 1.0 / np.sqrt(C)
        return {'x': jax.random.normal(ks[0], (B, H, W, C), dtype=jnp.float32), 'qkv_w': jax.random.uniform(ks[1], (3 * C, C), jnp.float32, -s, s), 'qkv_b': jax.random.uniform(ks[2], (3 * C,), jnp.float32, -s, s), 'proj_w': jax.random.uniform(ks[3], (C, C), jnp.float32, -s, s), 'proj_b': jax.random.uniform(ks[4], (C,), jnp.float32, -s, s)}
    _L0_tok_all = _L0_tok_setup()
    _L0_tok_in = {k: v for k, v in _L0_tok_all.items() if k in ('qkv_w', 'qkv_b', 'proj_w', 'proj_b')}
    del _L0_tok_all

    def _L0_attn_setup():
        import jax, jax.numpy as jnp
        import numpy as np
        import math
        B, N, DIM = (2, 1024, 64)
        NUM_HEADS = 8
        HEAD_DIM = DIM // NUM_HEADS
        WINDOW = 7

        def local_mask(seq_len: int, window_size: int=WINDOW) -> jnp.ndarray:
            grid = int(math.isqrt(seq_len))
            idx = jnp.arange(seq_len)
            row, col = (idx // grid, idx % grid)
            half = window_size // 2
            ok_row = jnp.abs(row[:, None] - row[None, :]) <= half
            ok_col = jnp.abs(col[:, None] - col[None, :]) <= half
            return ok_row & ok_col
        key = jax.random.key(seed)
        k1, k2, k3, k4 = jax.random.split(key, 4)
        x = jax.random.normal(k1, (B, N, DIM), dtype=jnp.float32)
        W_qkv = jax.random.normal(k2, (3 * DIM, DIM), dtype=jnp.float32) * DIM ** (-0.5)
        W_proj = jax.random.normal(k3, (DIM, DIM), dtype=jnp.float32) * DIM ** (-0.5)
        b_proj = jax.random.normal(k4, (DIM,), dtype=jnp.float32) * 0.01
        temperature = jnp.ones((1,), dtype=jnp.float32)
        return {'x': x, 'W_qkv': W_qkv, 'W_proj': W_proj, 'b_proj': b_proj, 'temperature': temperature}
    _L0_attn_all = _L0_attn_setup()
    _L0_attn_in = {k: v for k, v in _L0_attn_all.items() if k in ('W_qkv', 'W_proj', 'b_proj', 'temperature')}
    del _L0_attn_all

    def _L0_ffn_setup():
        import jax, jax.numpy as jnp
        import numpy as np
        B, T, IN_DIM = (64, 64, 64)
        HID, OUT_DIM = (128, 64)
        N_LAYERS, N_EXPERTS, N_SHARED = (2, 16, 1)
        key = jax.random.key(seed)
        ks = jax.random.split(key, 10)
        s = 0.02
        x = jax.random.normal(ks[0], (B, T, IN_DIM), dtype=jnp.float32)
        route_id = jax.random.randint(ks[1], (B,), 0, N_EXPERTS)
        Wi = jax.random.normal(ks[2], (HID, IN_DIM), dtype=jnp.float32) * s
        bi = jnp.zeros((HID,), dtype=jnp.float32)
        Wr = jax.random.normal(ks[3], (N_LAYERS, N_EXPERTS, HID, HID), dtype=jnp.float32) * s
        br = jax.random.normal(ks[4], (N_LAYERS, N_EXPERTS, HID), dtype=jnp.float32) * s
        Ws = jax.random.normal(ks[5], (N_LAYERS, N_SHARED, HID, HID), dtype=jnp.float32) * s
        bs = jax.random.normal(ks[6], (N_LAYERS, N_SHARED, HID), dtype=jnp.float32) * s
        Wo = jax.random.normal(ks[7], (OUT_DIM, HID), dtype=jnp.float32) * s
        bo = jnp.zeros((OUT_DIM,), dtype=jnp.float32)
        return {'x': x, 'route_id': route_id, 'Wi': Wi, 'bi': bi, 'Wr': Wr, 'br': br, 'Ws': Ws, 'bs': bs, 'Wo': Wo, 'bo': bo}
    _L0_ffn_all = _L0_ffn_setup()
    _L0_ffn_in = {k: v for k, v in _L0_ffn_all.items() if k in ('route_id', 'Wi', 'bi', 'Wr', 'br', 'Ws', 'bs', 'Wo', 'bo')}
    del _L0_ffn_all

    def _L1_attn_setup():
        import jax, jax.numpy as jnp
        import numpy as np
        EMBED_DIM = 64
        SEQ_LEN = 1024
        BATCH = 8
        ALPHA = 0.99
        key = jax.random.key(seed)
        k_x, k_w, k_b = jax.random.split(key, 3)
        x = jax.random.normal(k_x, (BATCH, SEQ_LEN, EMBED_DIM), dtype=jnp.float32)
        Wqkv = jax.random.normal(k_w, (EMBED_DIM, 3 * EMBED_DIM), dtype=jnp.float32) * EMBED_DIM ** (-0.5)
        bqkv = jax.random.normal(k_b, (3 * EMBED_DIM,), dtype=jnp.float32) * 0.02
        return {'x': x, 'Wqkv': Wqkv, 'bqkv': bqkv}
    _L1_attn_all = _L1_attn_setup()
    _L1_attn_in = {k: v for k, v in _L1_attn_all.items() if k in ('Wqkv', 'bqkv')}
    del _L1_attn_all

    def _L1_ffn_setup():
        import jax, jax.numpy as jnp
        import numpy as np
        B, H, E, IN, OUT = (1024, 1, 8, 64, 64)

        @jax.custom_vjp
        def bin_active(x):
            return jnp.sign(x)

        def _ba_fwd(x):
            return (jnp.sign(x), x)

        def _ba_bwd(x, g):
            return (g * (jnp.abs(x) <= 1.0).astype(g.dtype),)
        bin_active.defvjp(_ba_fwd, _ba_bwd)

        @jax.custom_vjp
        def bin_gate(x):
            return (x > 0.5).astype(x.dtype)

        def _bg_fwd(x):
            return ((x > 0.5).astype(x.dtype), None)

        def _bg_bwd(_, g):
            return (g,)
        bin_gate.defvjp(_bg_fwd, _bg_bwd)
        key = jax.random.key(seed)
        k1, k2, k3, k4, k5 = jax.random.split(key, 5)
        x = jax.random.normal(k1, (B, H, IN), dtype=jnp.float32)
        weight = jax.random.normal(k2, (H, E, IN, OUT), dtype=jnp.float32) * 0.05
        proj_w = jax.random.normal(k3, (E, IN), dtype=jnp.float32) * 0.05
        proj_b = jax.random.normal(k4, (E,), dtype=jnp.float32) * 0.05
        scale = jax.random.normal(k5, (H, 1, OUT), dtype=jnp.float32) * 0.1
        return {'x': x, 'weight': weight, 'proj_w': proj_w, 'proj_b': proj_b, 'scale': scale}
    _L1_ffn_all = _L1_ffn_setup()
    _L1_ffn_in = {k: v for k, v in _L1_ffn_all.items() if k in ('weight', 'proj_w', 'proj_b', 'scale')}
    del _L1_ffn_all
    return {'x': x, 'L0_tok_qkv_w': _L0_tok_in['qkv_w'], 'L0_tok_qkv_b': _L0_tok_in['qkv_b'], 'L0_tok_proj_w': _L0_tok_in['proj_w'], 'L0_tok_proj_b': _L0_tok_in['proj_b'], 'L0_attn_W_qkv': _L0_attn_in['W_qkv'], 'L0_attn_W_proj': _L0_attn_in['W_proj'], 'L0_attn_b_proj': _L0_attn_in['b_proj'], 'L0_attn_temperature': _L0_attn_in['temperature'], 'L0_ffn_route_id': _L0_ffn_in['route_id'], 'L0_ffn_Wi': _L0_ffn_in['Wi'], 'L0_ffn_bi': _L0_ffn_in['bi'], 'L0_ffn_Wr': _L0_ffn_in['Wr'], 'L0_ffn_br': _L0_ffn_in['br'], 'L0_ffn_Ws': _L0_ffn_in['Ws'], 'L0_ffn_bs': _L0_ffn_in['bs'], 'L0_ffn_Wo': _L0_ffn_in['Wo'], 'L0_ffn_bo': _L0_ffn_in['bo'], 'L1_attn_Wqkv': _L1_attn_in['Wqkv'], 'L1_attn_bqkv': _L1_attn_in['bqkv'], 'L1_ffn_weight': _L1_ffn_in['weight'], 'L1_ffn_proj_w': _L1_ffn_in['proj_w'], 'L1_ffn_proj_b': _L1_ffn_in['proj_b'], 'L1_ffn_scale': _L1_ffn_in['scale']}

def reference(x, L0_tok_qkv_w, L0_tok_qkv_b, L0_tok_proj_w, L0_tok_proj_b, L0_attn_W_qkv, L0_attn_W_proj, L0_attn_b_proj, L0_attn_temperature, L0_ffn_route_id, L0_ffn_Wi, L0_ffn_bi, L0_ffn_Wr, L0_ffn_br, L0_ffn_Ws, L0_ffn_bs, L0_ffn_Wo, L0_ffn_bo, L1_attn_Wqkv, L1_attn_bqkv, L1_ffn_weight, L1_ffn_proj_w, L1_ffn_proj_b, L1_ffn_scale):
    import jax
    import jax.numpy as jnp

    def _L0_tok_ref(x, qkv_w, qkv_b, proj_w, proj_b):
        import jax, jax.numpy as jnp
        import numpy as np
        DIM = 64
        NH = 8
        WH, WW = (8, 8)

        def _rope_axis(x, axis):
            half = x.shape[-1]
            inv_freq = 1.0 / 10000.0 ** (jnp.arange(0, half, 2, dtype=jnp.float32) / half)
            pos = jnp.arange(x.shape[axis], dtype=jnp.float32)
            ang = pos[:, None] * inv_freq
            cos, sin = (jnp.cos(ang), jnp.sin(ang))
            shape = [1, 1, 1, ang.shape[-1]]
            shape[axis] = ang.shape[0]
            cos = cos.reshape(shape).astype(x.dtype)
            sin = sin.reshape(shape).astype(x.dtype)
            x1, x2 = (x[..., 0::2], x[..., 1::2])
            r1 = x1 * cos - x2 * sin
            r2 = x1 * sin + x2 * cos
            return jnp.stack([r1, r2], axis=-1).reshape(x.shape)

        def _rope2(x):
            half = x.shape[-1] // 2
            return jnp.concatenate([_rope_axis(x[..., :half], 1), _rope_axis(x[..., half:], 2)], axis=-1)
        B, H, W, C = x.shape
        hd = C // NH
        N = WH * WW
        xw = x.reshape(B, H // WH, WH, W // WW, WW, C).transpose(0, 1, 3, 2, 4, 5).reshape(-1, N, C)
        qkv = xw @ qkv_w.T + qkv_b
        qkv = qkv.reshape(-1, N, 3, NH, hd).transpose(2, 0, 3, 1, 4)
        q, k, v = (qkv[0], qkv[1], qkv[2])
        q = _rope2(q.reshape(-1, WH, WW, hd)).reshape(-1, NH, N, hd)
        k = _rope2(k.reshape(-1, WH, WW, hd)).reshape(-1, NH, N, hd)
        scale = hd ** (-0.5)
        attn = jax.nn.softmax(q * scale @ jnp.swapaxes(k, -2, -1), axis=-1)
        out = (attn @ v).transpose(0, 2, 1, 3).reshape(-1, N, C)
        out = out.reshape(B, H // WH, W // WW, WH, WW, C).transpose(0, 1, 3, 2, 4, 5).reshape(B, H * W, C)
        return out @ proj_w.T + proj_b

    def _L0_attn_ref(x, W_qkv, W_proj, b_proj, temperature):
        import jax, jax.numpy as jnp
        import numpy as np
        import math
        B, N, DIM = (2, 1024, 64)
        NUM_HEADS = 8
        HEAD_DIM = DIM // NUM_HEADS
        WINDOW = 7

        def local_mask(seq_len: int, window_size: int=WINDOW) -> jnp.ndarray:
            grid = int(math.isqrt(seq_len))
            idx = jnp.arange(seq_len)
            row, col = (idx // grid, idx % grid)
            half = window_size // 2
            ok_row = jnp.abs(row[:, None] - row[None, :]) <= half
            ok_col = jnp.abs(col[:, None] - col[None, :]) <= half
            return ok_row & ok_col
        Bb, Nn, C = x.shape
        scale = HEAD_DIM ** (-0.5)
        qkv = (x @ W_qkv.T).reshape(Bb, Nn, 3, NUM_HEADS, HEAD_DIM)
        qkv = jnp.transpose(qkv, (2, 0, 3, 1, 4))
        q, k, v = (qkv[0], qkv[1], qkv[2])
        attn = jnp.einsum('bhqd,bhkd->bhqk', q, k) * (scale * temperature[0])
        mask = local_mask(Nn)
        attn = jnp.where(mask[None, None, :, :], attn, -jnp.inf)
        attn = jax.nn.softmax(attn, axis=-1)
        out = jnp.einsum('bhqk,bhkd->bhqd', attn, v)
        out = jnp.transpose(out, (0, 2, 1, 3)).reshape(Bb, Nn, C)
        return out @ W_proj.T + b_proj

    def _L0_ffn_ref(x, route_id, Wi, bi, Wr, br, Ws, bs, Wo, bo):
        import jax, jax.numpy as jnp
        import numpy as np
        B, T, IN_DIM = (64, 64, 64)
        HID, OUT_DIM = (128, 64)
        N_LAYERS, N_EXPERTS, N_SHARED = (2, 16, 1)
        flat = x.reshape(-1, x.shape[-1])
        n_tok = flat.shape[0]
        route = jnp.repeat(route_id, n_tok // route_id.shape[0])
        h = jax.nn.relu(flat @ Wi.T + bi)
        n_layers, n_experts = (Wr.shape[0], Wr.shape[1])
        for l in range(n_layers):
            shared = (jnp.einsum('nd,shd->snh', h, Ws[l]) + bs[l][:, None, :]).mean(axis=0)
            routed = jnp.zeros_like(h)
            for e in range(n_experts):
                ye = h @ Wr[l, e].T + br[l, e]
                routed = routed + jnp.where((route == e)[:, None], ye, 0.0)
            h = jax.nn.relu(shared + routed + h)
        out = h @ Wo.T + bo
        return out.reshape(*x.shape[:-1], out.shape[-1])

    def _L1_attn_ref(x, Wqkv, bqkv):
        import jax, jax.numpy as jnp
        import numpy as np
        EMBED_DIM = 64
        SEQ_LEN = 1024
        BATCH = 8
        ALPHA = 0.99
        bs, sl, d = x.shape
        qkv = x @ Wqkv + bqkv
        q, k, v = jnp.split(qkv, 3, axis=-1)
        i = jnp.arange(sl, dtype=jnp.float32)
        M = jnp.where(i[:, None] >= i[None, :], jnp.power(jnp.float32(ALPHA), i[:, None] - i[None, :]), 0.0)
        scores = jnp.einsum('bqd,bkd->bqk', q, k) / jnp.sqrt(jnp.float32(d))
        out = jnp.einsum('bqk,bkd->bqd', scores * M, v)
        return out

    def _L1_ffn_ref(x, weight, proj_w, proj_b, scale):
        import jax, jax.numpy as jnp
        import numpy as np
        B, H, E, IN, OUT = (1024, 1, 8, 64, 64)

        @jax.custom_vjp
        def bin_active(x):
            return jnp.sign(x)

        def _ba_fwd(x):
            return (jnp.sign(x), x)

        def _ba_bwd(x, g):
            return (g * (jnp.abs(x) <= 1.0).astype(g.dtype),)
        bin_active.defvjp(_ba_fwd, _ba_bwd)

        @jax.custom_vjp
        def bin_gate(x):
            return (x > 0.5).astype(x.dtype)

        def _bg_fwd(x):
            return ((x > 0.5).astype(x.dtype), None)

        def _bg_bwd(_, g):
            return (g,)
        bin_gate.defvjp(_bg_fwd, _bg_bwd)
        xh = jnp.transpose(x, (1, 0, 2))
        gate = jax.nn.sigmoid(jnp.einsum('hbi,ei->hbe', xh, proj_w) + proj_b)
        gate = bin_gate(gate)
        w = jnp.einsum('hbe,heio->hbio', gate, weight)
        xb = bin_active(xh)
        wb = bin_active(w)
        y = jnp.einsum('hbi,hbio->hbo', xb, wb)
        y = y * scale
        return jnp.transpose(y, (1, 0, 2))
    h = _L0_tok_ref(x, L0_tok_qkv_w, L0_tok_qkv_b, L0_tok_proj_w, L0_tok_proj_b)
    h = h + _L0_attn_ref(_layernorm(h, axis=-1), L0_attn_W_qkv, L0_attn_W_proj, L0_attn_b_proj, L0_attn_temperature)
    h = h + _L0_ffn_ref(_layernorm(h, axis=-1), L0_ffn_route_id, L0_ffn_Wi, L0_ffn_bi, L0_ffn_Wr, L0_ffn_br, L0_ffn_Ws, L0_ffn_bs, L0_ffn_Wo, L0_ffn_bo)
    h = h + _L1_attn_ref(_layernorm(h, axis=-1), L1_attn_Wqkv, L1_attn_bqkv)
    h = h + _L1_ffn_ref(_layernorm(h, axis=-1), L1_ffn_weight, L1_ffn_proj_w, L1_ffn_proj_b, L1_ffn_scale)
    return h

_drawn_inputs = setup_inputs


def setup_inputs(seed=0):
    import zlib

    import numpy as np

    out = dict(_drawn_inputs(seed))
    spreads = {'L0_ffn_bi': (0.0, 0.301), 'L0_ffn_bo': (0.0, 0.1)}
    factors = {'L0_attn_b_proj': 3.697,
     'L0_ffn_Wr': 6.292,
     'L0_ffn_br': 8.0,
     'L0_ffn_Ws': 5.34,
     'L0_ffn_bs': 8.0,
     'L1_ffn_weight': 8.0,
     'L1_ffn_proj_w': 8.0,
     'L1_ffn_proj_b': 27.645,
     'L1_ffn_scale': 8.0}
    for name, (base, spread) in spreads.items():
        noise = np.random.default_rng([zlib.crc32(name.encode()), seed]).standard_normal(out[name].shape)
        drawn = base * np.exp(spread * noise) if base else spread * noise
        out[name] = jnp.asarray(drawn.astype(out[name].dtype))
    for name, factor in factors.items():
        out[name] = (out[name] * factor).astype(out[name].dtype)
    return out
```

```python
from contextlib import ExitStack

import numpy as np
import concourse.bass as bass
from concourse import mybir

F32 = mybir.dt.float32
BF16 = mybir.dt.bfloat16
I32 = mybir.dt.int32
ALU = mybir.AluOpType
ACT = mybir.ActivationFunctionType
AX = mybir.AxisListType

P = 128
B, H, W, C = 4, 64, 64, 64
NH, HD = 8, 8
TOK = B * H * W
TILES = TOK // P
WIN = 8
QP = 4
NQ = QP * QP
HALF = 3
KS = QP + 2 * HALF
NKL = KS * KS
NKT = WIN * WIN
PW = W + 2 * HALF
CMOD = 12
NAUG = KS + CMOD + 1
BIG = 1.0e9
HID, NEXP, NLAY = 128, 16, 2
KL_ROWS = C + NAUG
NG = 8
EPS = 1e-5
ALPHA = 0.99
STRIPS = H // QP
GP = 4


def shape_tables():
    t = {}
    t["ident"] = np.eye(P, dtype=np.float32)
    ch = np.arange(C)
    d = ch % HD
    half = HD // 2
    freq = (1.0 / 10000.0 ** (np.arange(0, half, 2, dtype=np.float32) / half)).astype(np.float32)
    f = freq[(d % half) // 2]
    wpos = np.arange(WIN * W)
    pos = np.where((d < half)[:, None], (wpos // WIN % WIN)[None, :], (wpos % WIN)[None, :])
    ang = (pos.astype(np.float32) * f[:, None]).astype(np.float32)
    cos, sin = np.cos(ang), np.sin(ang) * np.where(d % 2 == 0, -1.0, 1.0)[:, None]
    scale = np.float32(HD ** -0.5)
    t["cos"] = np.concatenate([cos, cos * scale]).astype(np.float32)
    t["sin"] = np.concatenate([sin, sin * scale]).astype(np.float32)
    hq = np.arange(P)
    t["headmask"] = (hq[:, None] // NQ == ch[None, :] // HD).astype(np.float32)
    t["sel"] = (hq[:, None] % NQ == np.arange(NQ)[None, :]).astype(np.float32)
    t["onehot"] = np.repeat(np.eye(32, dtype=np.float32)[:, :, None], NKL, 2).reshape(32, -1)
    aug = np.zeros((STRIPS, NAUG, KS, PW), np.float32)
    for r in range(KS):
        aug[:, r, r, :] = 1
    for c in range(PW):
        aug[:, KS + c % CMOD, :, c] = 1
        if c < HALF or c >= PW - HALF:
            aug[:, KS + CMOD, :, c] = 1
    aug[0, KS + CMOD, :HALF, :] = 1
    aug[STRIPS - 1, KS + CMOD, KS - HALF:, :] = 1
    t["kaug"] = aug.reshape(STRIPS, NAUG, KS * PW)
    qa = np.zeros((NAUG, QP, W), np.float32)
    for r in range(QP):
        for kr in range(KS):
            if abs(kr - HALF - r) > HALF:
                qa[kr, r, :] = -BIG
    for c in range(W):
        j = c // QP
        for kc in range(KS):
            if abs(kc - HALF - c % QP) > HALF:
                qa[KS + (QP * j + kc) % CMOD, :, c] = -BIG
    qa[KS + CMOD] = -BIG
    qa = qa.reshape(NAUG, QP, W // QP, QP).transpose(0, 2, 1, 3).reshape(NAUG, W // QP, 1, NQ)
    t["qaug"] = np.repeat(qa, NH, 2).reshape(NAUG, -1)
    i = np.arange(P, dtype=np.float64)
    dm = np.where(i[None, :] >= i[:, None], ALPHA ** (i[None, :] - i[:, None]), 0.0) / np.sqrt(C)
    t["decay"] = dm.astype(np.float32)
    t["decay_q"] = np.tile((ALPHA ** (i + 1) / np.sqrt(C))[None, :], (C, 2)).astype(np.float32)
    t["decay_k"] = (ALPHA ** (P - 1 - i))[:, None].astype(np.float32)
    return t


def build(nc, a, out):
    ctx = ExitStack()
    with ctx:
        def sb(name, shape, dt=F32):
            return ctx.enter_context(nc.sbuf_tensor(name, shape, dt))

        def sem(name):
            return ctx.enter_context(nc.semaphore(name))

        bank = {n: ctx.enter_context(nc.psum_tensor("ps_" + n, [P, 512], F32))
                for n in ("T", "J1", "J2", "MX", "S0", "S1", "AV", "OT")}

        h = sb("h", [P, TILES, C])
        ident = sb("ident", [P, P])
        cos, sin = sb("cos", [P, 512]), sb("sin", [P, 512])
        headmask, sel = sb("headmask", [P, C]), sb("sel", [P, NQ])
        onehot_f, onehot = sb("onehot_f", [32, 32 * NKL]), sb("onehot", [32, 32 * NKL], BF16)
        decay, decay_q, decay_k = sb("decay", [P, P]), sb("decay_q", [C, 256]), sb("decay_k", [P, 1])
        w_qk, w_qk_swap, w_v1, w_p1 = sb("w_qk", [65, 128]), sb("w_qk_swap", [65, 128]), sb("w_v1", [65, C]), sb("w_p1", [65, C])
        w_q2, w_k2, w_v2, w_p2 = sb("w_q2", [C, C]), sb("w_k2", [C, C]), sb("w_v2", [C, C]), sb("w_p2", [65, C])
        temp = sb("temp", [C, 1])
        w_i = sb("w_i", [65, HID])
        experts = sb("experts", [P, NLAY, NEXP + 1, HID + 1])
        shared = sb("shared", [P, NLAY, HID + 1])
        w_o, b_o, ones_row = sb("w_o", [P, C]), sb("b_o", [1, C]), sb("ones_row", [1, P])
        w_q3, w_k3, w_kv3 = sb("w_q3", [65, C]), sb("w_k3", [65, C]), sb("w_kv3", [65, 128])
        w_gate = sb("w_gate", [65, 3 * NG])
        w_bin, w_rest = sb("w_bin", [P, C * C * NG // P]), sb("w_rest", [P, C * C * NG // P])
        w_3 = sb("w_3", [P, 3, C * C * NG // P], BF16)
        w_parts = sb("w_parts", [3 * NG, C * C], BF16)
        pair_sel = sb("pair_sel", [P, 2], BF16)
        pair_f = sb("pair_f", [P, 2])
        scale_bc = sb("scale_bc", [P, C])
        route_i, route_f, route_ok, route_x = sb("route_i", [1, 64], I32), sb("route_f", [1, 64]), sb("route_ok", [1, 64]), sb("route_x", [1, 64], I32)
        minus_half = sb("minus_half", [P, 4])
        zeros = sb("zeros", [C, HALF * PW])

        xin = sb("xin", [P, 4, C])
        xT = sb("xT", [65, 512])
        t_cos, t_sin, rot = sb("t_cos", [P, 512]), sb("t_sin", [P, 512]), sb("rot", [P, 512])
        qexp = sb("qexp", [P, NH * 512])
        q_blocks = qexp[:, :].rearrange("k (p h q) -> k p h q", h=NH, q=NQ)
        kpatch, xpatch = sb("kpatch", [KL_ROWS, 16 * NKL]), sb("xpatch", [C, 16 * NKL])
        kst, xst = sb("kst", [P, KS * PW]), sb("xst", [C, KS * PW])
        vsb = sb("vsb", [NKL, 16, C + 1])
        m_sb, mT = sb("m_sb", [P, 32]), sb("mT", [32, P], BF16)
        prob = sb("prob", [P, 2, 512])
        rec, selr, msk = sb("rec", [P, 2, GP]), sb("selr", [P, 2, GP * NQ]), sb("msk", [P, 2, GP * C])
        aT = sb("aT", [65, 512])
        stats, mv, veps, rstd = sb("stats", [P, 4, 6]), sb("mv", [P, 4, 2]), sb("veps", [P, 4]), sb("rstd", [P, 4])
        xn = sb("xn", [P, 4, C])
        xpad, kpad, q_sb = sb("xpad", [C, WIN * PW]), sb("kpad", [C, WIN * PW]), sb("q_sb", [C, 512])
        xnT = sb("xnT", [65, 256])
        hidT = sb("hidT", [P, 3, 256])
        w_exp = sb("w_exp", [P, NLAY, HID + 1])
        qk3, qd3 = sb("qk3", [C, 512]), sb("qd3", [C, 256])
        kd3, v3, sd3 = sb("kd3", [P, 2, C]), sb("v3", [P, 2, C]), sb("sd3", [P, 2, P])
        state = sb("state", [C, 2, C])
        xn2 = sb("xn2", [P, 2, 2, C])
        xb2 = sb("xb2", [P, 256], BF16)
        g3 = sb("g3", [3 * NG, 256], BF16)
        sgn, prod = sb("sgn", [P, 2, 1024], BF16), sb("prod", [P, 2, 1024], BF16)
        ys, yo = sb("ys", [P, 2, C]), sb("yo", [P, 2, C])

        kx_d = nc.dram_tensor("kx_d", (B, 2, C, PW * PW), F32, kind="Internal").ap()
        qs_d = nc.dram_tensor("qs_d", (C, TOK), F32, kind="Internal").ap()
        x_v = a["x"].rearrange("b (t y) w c -> (y w) (b t) c", y=2)
        o_v = out.rearrange("b (t p) c -> p (b t) c", p=P)

        s_w = sem("weights_loaded")
        s_const = sem("constants_made")
        s_prep = sem("experts_combined")
        s_route = sem("routes_ready")
        s_parts = sem("gate_weights_split")
        s_moved = sem("gate_weight_parts_moved")

        def named(prefix, *names):
            return {n: sem(prefix + "_" + n) for n in names}

        def wait(eng, semaphore, count):
            eng.wait_ge(semaphore, count + 1)

        s_settled = sem("settled")

        def settle(eng):
            eng.sem_inc(s_settled, 1)

        core = ("max_scores", "max_done", "maxT", "negmax", "scores", "exp_done", "av_done", "rec_done",
                "norm_done", "sel_done", "attn_out", "v_ps", "v_sb", "q_in", "k_in", "x_patch", "k_patch", "proj", "h_done")
        T1 = named("tok", "x_in", "xT_ps", "xT_sb", "qk_ps", "rope_mul", "rope", *core)
        T2 = named("loc", *core)
        L = named("pre", "stats", "mv", "veps", "rstd", "xn", "xT_ps", "xT_sb", "k_ps", "q_ps", "k_sb", "q_sb", "stored", "padded")
        FF = named("ffn", "stats", "mv", "veps", "rstd", "xn", "xT_ps", "xT_sb", "w_in", "hid_ps", "hid_sb", "out_ps", "h_done")
        RT = named("ret", "stats", "mv", "veps", "rstd", "xn", "xT_ps", "xT_sb", "qk_ps", "qk_sb", "kv_ps", "kd", "v", "qd", "s_ps",
                   "sd", "kv_sum", "state", "reset", "out_ps", "h_done")
        BN = named("bin", "stats", "mv", "veps", "rstd", "xn", "xT_ps", "xb", "xT_sb", "g_ps", "gates", "w_ps", "sign", "prod",
                   "y_part", "y_ps", "y_scaled", "y", "stored")

        def cfg(s, nk, kdim, rows, keys, qview, vkeys, npatch):
            return dict(s=s, nk=nk, kdim=kdim, rows=rows, keys=keys, q=qview, v=vkeys, np=npatch, ng=npatch // GP)

        KL = C + NAUG

        def operands(q, k, rows, nk):
            def of(buf, n, at, narrow):
                if narrow:
                    return buf[0:rows, at * n:(at + 1) * n].bitcast(BF16).rearrange("p (n e) -> p n e", e=2)[:, :, 1]
                return buf[0:rows, at * n:(at + 1) * n]
            return (lambda p, narrow: of(q, P, p, narrow)), (lambda p, narrow: of(k, nk, NKEY[nk](p), narrow))

        NKEY = {NKT: lambda p: p // 4, NKL: lambda p: p}
        tok_q, tok_k = operands(qexp, rot, C, NKT)
        loc_q, loc_k = operands(qexp, kpatch, KL, NKL)

        def tok_at(p):
            return QP * (p // 2 % 2), WIN * (p // 4) + QP * (p % 2)

        def loc_at(p):
            return 0, QP * p

        TOKC = dict(nv=1, s=T1, nk=NKT, np=32, ng=8, q=tok_q, k=tok_k, v=lambda p: vsb[0:NKT, p // 4, :], at=tok_at)
        LOCC = dict(nv=2, s=T2, nk=NKL, np=16, ng=4, q=loc_q, k=loc_k, v=lambda p: vsb[0:NKL, p, :], at=loc_at)
        onehot_v = onehot[:, :].rearrange("k (p n) -> k p n", p=32)
        S = [bank["S0"], bank["S1"]]
        NT = TOK // 512
        NS = TOK // 256

        block = ctx.enter_context(nc.Block())

        @block.sync
        def _(sp):
            loads = [(ident[:, :], a["ident"]), (cos[:, :], a["cos"]), (sin[:, :], a["sin"]), (headmask[:, :], a["headmask"]),
                     (sel[:, :], a["sel"]), (onehot_f[:, :], a["onehot"]), (decay[:, :], a["decay"]), (decay_q[:, :], a["decay_q"]),
                     (decay_k[:, :], a["decay_k"]), (w_qk[:, :], a["w_qk"]), (w_qk_swap[:, :], a["w_qk_swap"]), (w_v1[:, :], a["w_v1"]),
                     (w_p1[:, :], a["w_p1"]), (w_q2[:, :], a["w_q2"]), (w_k2[:, :], a["w_k2"]), (w_v2[:, :], a["w_v2"]),
                     (w_p2[:, :], a["w_p2"]), (temp[:, :], a["temp"].broadcast_to((C, 1))), (w_i[:, :], a["w_i"]),
                     (shared[:, :, :], a["shared"]), (w_o[:, :], a["w_o"]), (b_o[:, :], a["b_o"]),
                     (w_q3[:, :], a["w_q3"]), (w_k3[:, :], a["w_k3"]), (w_kv3[:, :], a["w_kv3"]), (w_gate[:, :], a["w_gate"]),
                     (w_bin[:, :], a["w_bin"]), (pair_f[:, :], a["pair"]), (scale_bc[:, :], a["scale"].broadcast_to((P, C))),
                     (route_i[:, :], a["route"]), (experts[:, :, 0:NEXP, :], a["experts"])]
            for stage in (T1, T2, L, FF, RT, BN):
                for signal in stage.values():
                    sp.sem_inc(signal, 1)
            for dst, src in loads:
                sp.dma_start(dst, src).then_inc(s_w, 16)
            assert len(loads) == NLOADS
            with sp.Fori(0, NT) as i:
                wait(sp, T1["xT_ps"], i)
                sp.dma_start(xin[:, :, :], x_v[:, bass.ds(i * 4, 4), :]).then_inc(T1["x_in"], 16)
                wait(sp, T1["rope"], (i + 1) * 3)
                wait(sp, T1["scores"], i * TOKC["ng"])
                for n in range(NH):
                    sp.dma_start(q_blocks[n * HD:(n + 1) * HD, :, n, :],
                                 rot[C + n * HD:C + (n + 1) * HD, :].rearrange("d (p q) -> d p q", q=NQ)).then_inc(T1["q_in"], 16)
            sp.wait_ge(s_const, NCONST)
            for b in range(B):
                for j in range(2):
                    for at in (0, (PW - HALF) * PW):
                        sp.dma_start(kx_d[b, j, :, at:at + HALF * PW], zeros[:, :]).then_inc(L["padded"], 16)
            with sp.Fori(0, B) as b:
                with sp.Fori(0, WIN) as w:
                    i = b * WIN + w
                    dst = kx_d.rearrange("b j c n -> (b j) c n")
                    wait(sp, L["xT_sb"], i + 1 + 1)
                    settle(sp)
                    wait(sp, L["k_sb"], i + 1)
                    settle(sp)
                    wait(sp, L["q_sb"], (i + 1) * 2)
                    settle(sp)
                    sp.dma_start(dst[bass.ds(b * 2 + 1, 1), :, bass.ds((w * WIN + HALF) * PW, WIN * PW)].rearrange("a c n -> (a c) n"),
                                 xpad[:, :]).then_inc(L["stored"], 16)
                    sp.dma_start(dst[bass.ds(b * 2, 1), :, bass.ds((w * WIN + HALF) * PW, WIN * PW)].rearrange("a c n -> (a c) n"),
                                 kpad[:, :]).then_inc(L["stored"], 16)
                    sp.dma_start(qs_d[:, bass.ds(i * 512, 512)], q_sb[:, :]).then_inc(L["stored"], 16)
            wait(sp, L["stored"], 48 * NT)
            wait(sp, L["padded"], 16 * 4 * B)
            wait(sp, T1["scores"], NT * TOKC["ng"])
            sp.wait_ge(s_const, NCONST + 1)
            sp.dma_start(qexp[C:KL, 0:NH * 256], a["qaug"]).then_inc(T2["q_in"], 16)
            with sp.Fori(0, B) as b:
                with sp.Fori(0, STRIPS) as s:
                    i = b * STRIPS + s
                    src = kx_d.rearrange("b j c n -> (b j) c n")
                    wait(sp, T2["x_patch"], i)
                    settle(sp)
                    sp.dma_start(xst[:, :], src[bass.ds(b * 2 + 1, 1), :, bass.ds(s * (QP * PW), KS * PW)].rearrange("a c n -> (a c) n")).then_inc(T2["k_in"], 16)
                    wait(sp, T2["k_patch"], i)
                    settle(sp)
                    sp.dma_start(kst[0:C, :], src[bass.ds(b * 2, 1), :, bass.ds(s * (QP * PW), KS * PW)].rearrange("a c n -> (a c) n")).then_inc(T2["k_in"], 16)
                    sp.dma_start(kst[C:KL, :], a["kaug"][bass.ds(s, 1), :, :].rearrange("a c n -> (a c) n")).then_inc(T2["k_in"], 16)
                    wait(sp, T2["scores"], i * LOCC["ng"])
                    for n in range(NH):
                        sp.dma_start(q_blocks[n * HD:(n + 1) * HD, 0:16, n, :],
                                     qs_d[n * HD:(n + 1) * HD, bass.ds(i * 256, 256)].rearrange("d (p q) -> d p q", q=NQ)).then_inc(T2["q_in"], 16)
            sp.wait_ge(s_prep, 2)
            sp.wait_ge(s_route, 4)
            with sp.Fori(0, NS) as i:
                wait(sp, FF["hid_sb"], i * 3)
                settle(sp)
                e = sp.value_load(route_x[0:1, bass.ds(i, 1)], min_val=0, max_val=NEXP)
                sp.dma_start(w_exp[:, :, :], experts[:, :, bass.ds(e, 1), :].rearrange("p l a n -> p l (a n)")).then_inc(FF["w_in"], 16)
            sp.wait_ge(s_parts, 5)
            for k in range(3):
                for g in range(NG):
                    r = P // NG
                    sp.dma_start(w_parts[k * NG + g:k * NG + g + 1, :].rearrange("a (r n) -> a r n", r=r), w_3[g * r:(g + 1) * r, k:k + 1, :]).then_inc(s_moved, 16)
            with sp.Fori(0, NS) as i:
                wait(sp, BN["y"], i + 1)
                sp.dma_start(o_v[:, bass.ds(i * 2, 2), :], yo[:, :, :]).then_inc(BN["stored"], 16)
            wait(sp, BN["stored"], 16 * NS)

        @block.gpsimd
        def _(gp):
            fills = [(xT[C:C + 1, :], 1.0), (aT[C:C + 1, :], 1.0), (xnT[C:C + 1, :], 1.0), (ones_row[:, :], 1.0), (minus_half[:, :], -0.5),
                     (zeros[:, :], 0.0), (xpad[:, :], 0.0), (kpad[:, :], 0.0), (vsb[:, :, :], 1.0), (qexp[:, :], 0.0),
                     (experts[:, :, NEXP:NEXP + 1, :], 0.0)]
            assert len(fills) == NCONST
            for n, (dst, value) in enumerate(fills):
                if n:
                    gp.wait_ge(s_const, n)
                gp.memset(dst, value).then_inc(s_const, 1)
            gp.wait_ge(s_const, NCONST)
            wait(gp, T1["scores"], NT * TOKC["ng"])
            gp.memset(qexp[:, :], 0.0).then_inc(s_const, 1)

            gp.wait_ge(s_const, NCONST + 1)

            def patches(buf, n):
                v = buf[0:n, :]
                return bass.AP(v.tensor, v.offset, [list(v.ap[0]), [QP, 16], [PW, KS], [1, KS]])

            def inv_std(q, i, n):
                wait(gp, q["rstd"], i)
                wait(gp, q["veps"], i + 1)
                gp.tensor_tensor(rstd[:, 0:n], veps[:, 0:n], minus_half[:, 0:n], ALU.pow).then_inc(q["rstd"], 1)

            with gp.Fori(0, NT) as i:
                inv_std(L, i, 4)
            with gp.Fori(0, NS) as i:
                wait(gp, T2["k_in"], (i + 1) * 48)
                wait(gp, T2["k_patch"], i)
                wait(gp, T2["v_ps"], i * 2)
                settle(gp)
                gp.tensor_copy(xpatch[:, :].rearrange("c (p r w) -> c p r w", p=16, r=KS), patches(xst, C)).then_inc(T2["x_patch"], 1)
                wait(gp, T2["scores"], i * LOCC["ng"])
                settle(gp)
                wait(gp, T2["x_patch"], i + 1)
                settle(gp)
                gp.tensor_copy(kpatch[:, :].rearrange("c (p r w) -> c p r w", p=16, r=KS), patches(kst, KL)).then_inc(T2["k_patch"], 1)
            for q in (FF, RT, BN):
                with gp.Fori(0, NS) as i:
                    inv_std(q, i, 2)

        @block.tensor
        def _(pe):
            def attention(c, i):
                q, nk, ng = c["s"], c["nk"], c["ng"]
                for g in range(ng):
                    wait(pe, q["max_done"], i * ng + g)
                    for u in range(GP):
                        mm = pe.matmul(bank["MX"][:, u * nk:(u + 1) * nk], c["q"](g * GP + u, True), c["k"](g * GP + u, True),
                                       start=True, stop=True)
                    mm.then_inc(q["max_scores"], 1)
                wait(pe, q["max_done"], (i + 1) * ng)
                pe.transpose(bank["T"][0:c["np"], 0:P], m_sb[:, 0:c["np"]], ident[:, :]).then_inc(q["maxT"], 1)
                wait(pe, q["negmax"], i + 1)

                def scores(g):
                    wait(pe, q["exp_done"], i * ng + g + 1)
                    settle(pe)
                    for u in range(GP):
                        o = S[g % 2][0:nk, u * P:(u + 1) * P]
                        pe.matmul(o, c["k"](g * GP + u, False), c["q"](g * GP + u, False), start=True, stop=False)
                        mm = pe.matmul(o, onehot_v[0:c["np"], g * GP + u, 0:nk], mT[0:c["np"], :], start=False, stop=True)
                    mm.then_inc(q["scores"], 1)

                def values(g):
                    wait(pe, q["exp_done"], i * ng + g + 3)
                    wait(pe, q["norm_done"], (i * ng + g) * 2)
                    for u in range(GP):
                        mm = pe.matmul(bank["AV"][:, u * (C + 1):(u + 1) * (C + 1)], prob[0:nk, g % 2, u * P:(u + 1) * P],
                                       c["v"](g * GP + u), start=True, stop=True)
                    mm.then_inc(q["av_done"], 1)

                def select(g):
                    wait(pe, q["norm_done"], (i * ng + g + 1) * 2)
                    for u in range(GP):
                        p = g * GP + u
                        r, w = c["at"](p)
                        o = bank["OT"][0:C, :].rearrange("c (r w) -> c r w", w=W)[:, r:r + QP, w:w + QP]
                        mm = pe.matmul(o, msk[:, g % 2, u * C:(u + 1) * C], selr[:, g % 2, u * NQ:(u + 1) * NQ], start=True, stop=True)
                    mm.then_inc(q["sel_done"], 1)

                for g in range(ng + 2):
                    if g < ng:
                        scores(g)
                    if 1 <= g <= ng:
                        if g == 1:
                            wait(pe, q["v_sb"], (i + 1) * c["nv"])
                        values(g - 1)
                    if g >= 2:
                        select(g - 2)

            def project(q, i, n, w):
                wait(pe, q["attn_out"], i + 1)
                wait(pe, q["h_done"], i)
                for t in range(n):
                    mm = pe.matmul(bank["J2"][:, t * C:(t + 1) * C], aT[:, t * P:(t + 1) * P], w[:, :], start=True, stop=True)
                mm.then_inc(q["proj"], 1)

            def turn(src, width, n, q, k):
                settle(pe)
                for t in range(n):
                    mm = pe.transpose(bank["T"][0:width, t * P:(t + 1) * P], src(t), ident[:, :])
                mm.then_inc(q[k], 1)

            pe.wait_ge(s_w, 16 * NLOADS)
            pe.wait_ge(s_const, NCONST)
            pe.wait_ge(s_prep, 3)
            with pe.Fori(0, NT) as i:
                wait(pe, T1["x_in"], (i + 1) * 16)
                wait(pe, T1["negmax"], i)
                turn(lambda t: xin[:, t, :], C, 4, T1, "xT_ps")
                wait(pe, T1["xT_sb"], i + 1)
                wait(pe, T1["h_done"], i)
                pe.matmul(bank["J1"][:, :], w_qk[:, :], xT[:, :], start=True, stop=True)
                pe.matmul(bank["J2"][:, :], w_qk_swap[:, :], xT[:, :], start=True, stop=True).then_inc(T1["qk_ps"], 1)
                wait(pe, T1["attn_out"], i)
                for n in range(8):
                    mm = pe.matmul(bank["OT"][0:NKT, n * C:(n + 1) * C], xT[:, n * NKT:(n + 1) * NKT], w_v1[:, :], start=True, stop=True)
                mm.then_inc(T1["v_ps"], 1)
                wait(pe, T1["v_sb"], i + 1)
                wait(pe, T1["q_in"], (i + 1) * 16 * NH)
                wait(pe, T1["rope"], (i + 1) * 3)
                attention(TOKC, i)
                project(T1, i, 4, w_p1)
            with pe.Fori(0, NT) as i:
                wait(pe, L["xn"], (i + 1) * 4)
                turn(lambda t: xn[:, t, :], C, 4, L, "xT_ps")
                wait(pe, L["xT_sb"], i + 2)
                wait(pe, L["k_sb"], i)
                wait(pe, L["q_sb"], i * 2)
                xw = xpad[:, :].rearrange("c (r w) -> c r w", w=PW)[:, :, HALF:HALF + W]
                settle(pe)
                pe.matmul(bank["J1"][0:C, :], w_k2[:, :], xw, start=True, stop=True).then_inc(L["k_ps"], 1)
                pe.matmul(bank["J2"][0:C, :], w_q2[:, :], xw, start=True, stop=True).then_inc(L["q_ps"], 1)
            with pe.Fori(0, NS) as i:
                wait(pe, T2["x_patch"], i + 1)
                wait(pe, T2["k_patch"], i + 1)
                wait(pe, T2["q_in"], (i + 1) * 16 * NH + 16)
                for hf in range(2):
                    if hf == 0:
                        wait(pe, T2["attn_out"], i)
                    else:
                        wait(pe, T2["v_sb"], i * 2 + 1)
                    for u in range(8):
                        p = hf * 8 + u
                        mm = pe.matmul(bank["OT"][0:NKL, u * C:(u + 1) * C], xpatch[:, p * NKL:(p + 1) * NKL], w_v2[:, :], start=True, stop=True)
                    mm.then_inc(T2["v_ps"], 1)
                wait(pe, T2["v_sb"], i * 2 + 2)
                attention(LOCC, i)
                project(T2, i, 2, w_p2)
            with pe.Fori(0, NS) as i:
                wait(pe, FF["xn"], (i + 1) * 2)
                turn(lambda t: xn[:, t, :], C, 2, FF, "xT_ps")
                wait(pe, FF["xT_sb"], i + 1)
                pe.matmul(bank["J1"][:, 0:256], w_i[:, :], xnT[:, :], start=True, stop=True).then_inc(FF["hid_ps"], 1)
                wait(pe, FF["w_in"], (i + 1) * 16)
                for l in range(NLAY):
                    wait(pe, FF["hid_sb"], i * 3 + l + 1)
                    pe.matmul(bank["J2" if l == 0 else "J1"][:, 0:256], w_exp[:, l, 0:HID], hidT[:, l, :], start=True, stop=True).then_inc(FF["hid_ps"], 1)
                wait(pe, FF["hid_sb"], i * 3 + 3)
                wait(pe, FF["h_done"], i)
                for t in range(2):
                    pe.matmul(bank["AV"][:, t * C:(t + 1) * C], hidT[:, 2, t * P:(t + 1) * P], w_o[:, :], start=True, stop=False)
                    mm = pe.matmul(bank["AV"][:, t * C:(t + 1) * C], ones_row[:, :], b_o[:, :], start=False, stop=True)
                mm.then_inc(FF["out_ps"], 1)
            with pe.Fori(0, B) as b, pe.Fori(0, STRIPS) as s:
                i = b * STRIPS + s
                wait(pe, RT["xn"], (i + 1) * 2)
                turn(lambda t: xn[:, t, :], C, 2, RT, "xT_ps")
                wait(pe, RT["xT_sb"], i + 1)
                pe.matmul(bank["J2"][0:C, 0:256], w_q3[:, :], xnT[:, :], start=True, stop=True)
                pe.matmul(bank["J2"][0:C, 256:512], w_k3[:, :], xnT[:, :], start=True, stop=True).then_inc(RT["qk_ps"], 1)
                for t in range(2):
                    mm = pe.matmul(bank["J1"][:, t * P:(t + 1) * P], xnT[:, t * P:(t + 1) * P], w_kv3[:, :], start=True, stop=True)
                mm.then_inc(RT["kv_ps"], 1)
                wait(pe, RT["qk_sb"], i + 1)
                for t in range(2):
                    mm = pe.matmul(bank["MX"][:, t * P:(t + 1) * P], qk3[:, 256 + t * P:256 + (t + 1) * P], qk3[:, t * P:(t + 1) * P], start=True, stop=True)
                mm.then_inc(RT["s_ps"], 1)
                wait(pe, RT["kd"], i + 1)
                wait(pe, RT["v"], i + 1)
                wait(pe, RT["sd"], i + 1)
                wait(pe, RT["qd"], i + 1)
                wait(pe, RT["reset"], b + 1)
                wait(pe, RT["h_done"], i)
                for t in range(2):
                    wait(pe, RT["state"], i * 2 + t)
                    pe.matmul(bank["OT"][0:C, 0:C], kd3[:, t, :], v3[:, t, :], start=True, stop=True).then_inc(RT["kv_sum"], 1)
                    pe.matmul(bank["AV"][:, t * C:(t + 1) * C], sd3[:, t, :], v3[:, t, :], start=True, stop=False)
                    mm = pe.matmul(bank["AV"][:, t * C:(t + 1) * C], qd3[:, t * P:(t + 1) * P], state[:, t, :], start=False, stop=True)
                mm.then_inc(RT["out_ps"], 1)
            pe.wait_ge(s_moved, 16 * 3 * NG + 2)
            with pe.Fori(0, NS) as i:
                wait(pe, BN["xn"], (i + 1) * 2)
                turn(lambda t: xn2[:, t, :, :], P, 2, BN, "xT_ps")
                wait(pe, BN["xT_sb"], i + 1)
                pe.matmul(bank["J1"][0:3 * NG, 0:256], w_gate[:, :], xnT[:, :], start=True, stop=True).then_inc(BN["g_ps"], 1)
                wait(pe, BN["gates"], i + 1)
                pairs = [(bank["J2"], bank["MX"]), (S[0], S[1])]

                def reduce(k):
                    wait(pe, BN["prod"], i * 8 + k + 1)
                    for u in range(4):
                        for t in range(2):
                            mm = pe.matmul(bank["AV"][:, t * C + (k * 4 + u) * 2:t * C + (k * 4 + u) * 2 + 2],
                                           prod[:, k % 2, u * 256 + t * P:u * 256 + (t + 1) * P], pair_sel[:, :], start=True, stop=True)
                    mm.then_inc(BN["y_part"], 1)

                for k in range(8):
                    wait(pe, BN["sign"], i * 8 + k + 1)
                    for u in range(4):
                        mm = pe.matmul(pairs[k % 2][u // 2][:, (u % 2) * 256:(u % 2) * 256 + 256],
                                       w_parts[:, (k * 4 + u) * P:(k * 4 + u + 1) * P], g3[:, :], start=True, stop=True)
                    mm.then_inc(BN["w_ps"], 1)
                    if k == 0:
                        wait(pe, BN["y_scaled"], i)
                    else:
                        reduce(k - 1)
                reduce(7)

        @block.scalar
        def _(act):
            def neg_max(c, i):
                q = c["s"]
                wait(act, q["maxT"], i + 1)
                act.activation(mT[0:c["np"], :], bank["T"][0:c["np"], 0:P], ACT.Copy, scale=-1.0).then_inc(q["negmax"], 1)

            def attention(c, i):
                q, nk, ng = c["s"], c["nk"], c["ng"]
                neg_max(c, i)
                for g in range(ng):
                    wait(act, q["scores"], i * ng + g + 1)
                    wait(act, q["av_done"], i * ng + g + 1)
                    act.activation(prob[0:nk, g % 2, :], S[g % 2][0:nk, :], ACT.Exp).then_inc(q["exp_done"], 1)
                wait(act, q["sel_done"], (i + 1) * ng + 2)
                n = c["np"] * NQ
                act.activation(aT[0:C, 0:n], bank["OT"][0:C, 0:n], ACT.Copy).then_inc(q["attn_out"], 1)

            act.wait_ge(s_w, 16 * NLOADS)
            act.wait_ge(s_const, NCONST)
            act.sem_inc(T1["exp_done"], 2)
            act.sem_inc(T2["exp_done"], 2)
            act.sem_inc(BN["sign"], 2)
            act.sem_inc(L["xT_sb"], 1)
            with act.Fori(0, NT) as i:
                wait(act, T1["xT_ps"], i + 1)
                act.activation(xT[0:C, :].rearrange("c (n r w) -> c n r w", n=8, r=WIN),
                               bank["T"][0:C, :].rearrange("c (r n w) -> c n r w", n=8, r=WIN), ACT.Copy).then_inc(T1["xT_sb"], 1)
                wait(act, T1["v_ps"], i + 1)
                act.activation(vsb[0:NKT, 0:8, 0:C], bank["OT"][0:NKT, :].rearrange("p (n c) -> p n c", c=C), ACT.Copy).then_inc(T1["v_sb"], 1)
                attention(TOKC, i)
            with act.Fori(0, NT) as i:
                wait(act, L["xT_ps"], i + 1)
                wait(act, L["stored"], i * 48)
                act.activation(xpad[:, :].rearrange("c (r w) -> c r w", w=PW)[:, :, HALF:HALF + W],
                               bank["T"][0:C, :].rearrange("c (r w) -> c r w", w=W), ACT.Copy).then_inc(L["xT_sb"], 1)
                wait(act, L["k_ps"], i + 1)
                act.activation(kpad[:, :].rearrange("c (r w) -> c r w", w=PW)[:, :, HALF:HALF + W],
                               bank["J1"][0:C, :].rearrange("c (r w) -> c r w", w=W), ACT.Copy).then_inc(L["k_sb"], 1)
            with act.Fori(0, NS) as i:
                for hf in range(2):
                    wait(act, T2["v_ps"], i * 2 + hf + 1)
                    act.activation(vsb[:, hf * 8:hf * 8 + 8, 0:C], bank["OT"][0:NKL, :].rearrange("p (n c) -> p n c", c=C), ACT.Copy).then_inc(T2["v_sb"], 1)
                attention(LOCC, i)
            with act.Fori(0, NS) as i:
                wait(act, FF["xT_ps"], i + 1)
                act.activation(xnT[0:C, :], bank["T"][0:C, 0:256], ACT.Copy).then_inc(FF["xT_sb"], 1)
                wait(act, FF["out_ps"], i)
                wait(act, FF["hid_ps"], i * 3 + 1)
                act.activation(hidT[:, 0, :], bank["J1"][:, 0:256], ACT.Relu).then_inc(FF["hid_sb"], 1)
                for l in range(NLAY):
                    wait(act, FF["hid_ps"], i * 3 + l + 2)
                    act.activation(hidT[:, l + 1, :], bank["J2" if l == 0 else "J1"][:, 0:256], ACT.Relu,
                                   bias=w_exp[:, l, HID:HID + 1]).then_inc(FF["hid_sb"], 1)
            with act.Fori(0, NS) as i:
                wait(act, RT["xT_ps"], i + 1)
                act.activation(xnT[0:C, :], bank["T"][0:C, 0:256], ACT.Copy).then_inc(RT["xT_sb"], 1)
                wait(act, RT["qk_ps"], i + 1)
                act.activation(qk3[:, :], bank["J2"][0:C, :], ACT.Copy).then_inc(RT["qk_sb"], 1)
                wait(act, RT["kv_ps"], i + 1)
                wait(act, RT["kd"], i + 1)
                act.activation(v3[:, :, :], bank["J1"][:, 0:256].rearrange("p (t n) -> p t n", t=2)[:, :, C:2 * C], ACT.Copy).then_inc(RT["v"], 1)
            with act.Fori(0, NS) as i:
                wait(act, BN["xT_ps"], i + 1)
                act.activation(xnT[0:C, :], bank["T"][0:C, 0:256], ACT.Copy).then_inc(BN["xT_sb"], 1)
                act.activation(xb2[:, :], bank["T"][:, 0:256], ACT.Sign).then_inc(BN["xb"], 1)
                pairs = [(bank["J2"], bank["MX"]), (S[0], S[1])]
                for k in range(8):
                    wait(act, BN["w_ps"], i * 8 + k + 1)
                    wait(act, BN["prod"], i * 8 + k)
                    for u in range(2):
                        op = act.activation(sgn[:, k % 2, u * 512:(u + 1) * 512], pairs[k % 2][u][:, :], ACT.Sign)
                    op.then_inc(BN["sign"], 1)

        @block.vector
        def _(dve):
            def attention(c, i):
                q, nk, ng = c["s"], c["nk"], c["ng"]
                wait(dve, q["maxT"], i)
                for g in range(ng):
                    wait(dve, q["max_scores"], i * ng + g + 1)
                    dve.tensor_reduce(m_sb[:, g * GP:(g + 1) * GP], bank["MX"][:, 0:GP * nk].rearrange("p (u n) -> p u n", u=GP),
                                      AX.X, ALU.max).then_inc(q["max_done"], 1)
                for g in range(ng):
                    v = bank["AV"][:, 0:GP * (C + 1)].rearrange("p (u n) -> p u n", u=GP)
                    wait(dve, q["av_done"], i * ng + g + 3)
                    wait(dve, q["sel_done"], i * ng + g + 1)
                    dve.reciprocal(rec[:, g % 2, :], v[:, :, C]).then_inc(q["rec_done"], 1)
                    dve.tensor_tensor(msk[:, g % 2, :].rearrange("p (u n) -> p u n", u=GP), v[:, :, 0:C],
                                      headmask[:, :].rearrange("p (a n) -> p a n", a=1).broadcast_to((P, GP, C)), ALU.mult).then_inc(q["norm_done"], 1)
                    wait(dve, q["rec_done"], i * ng + g + 1)
                    dve.tensor_tensor(selr[:, g % 2, :].rearrange("p (u n) -> p u n", u=GP),
                                      sel[:, :].rearrange("p (a n) -> p a n", a=1).broadcast_to((P, GP, NQ)),
                                      rec[:, g % 2, :].rearrange("p (u a) -> p u a", a=1).broadcast_to((P, GP, NQ)), ALU.mult).then_inc(q["norm_done"], 1)

            def layer_norm(q, i, n, src, dst):
                for t in range(n):
                    dve.bn_stats(stats[:, t, :], src(t)).then_inc(q["stats"], 1)
                for t in range(n):
                    wait(dve, q["stats"], i * n + t + 1)
                    settle(dve)
                    dve.bn_aggr(mv[:, t, :], stats[:, t, :]).then_inc(q["mv"], 1)
                wait(dve, q["mv"], (i + 1) * n)
                dve.tensor_scalar(veps[:, 0:n], mv[:, 0:n, 1], EPS, None, ALU.add).then_inc(q["veps"], 1)
                wait(dve, q["rstd"], i + 1)
                wait(dve, q["xT_ps"], i)
                for t in range(n):
                    s = src(t)
                    d = dst(t)
                    if len(d.shape) == 3:
                        s = s.rearrange("p (a c) -> p a c", a=1).broadcast_to((P, 2, C))
                    dve.tensor_scalar(d, s, mv[:, t, 0:1], rstd[:, t:t + 1], ALU.subtract, ALU.mult).then_inc(q["xn"], 1)

            def rows(t0, n):
                return h[:, bass.ds(t0, n), :]

            def row(t0):
                return lambda t: h[:, bass.ds(t0 + t, 1), :].rearrange("p a c -> p (a c)")

            dve.sem_inc(T1["av_done"], 2)
            dve.sem_inc(T2["av_done"], 2)
            dve.sem_inc(T1["sel_done"], 2)
            dve.sem_inc(T2["sel_done"], 2)
            dve.wait_ge(s_w, 16 * NLOADS)
            dve.wait_ge(s_const, NCONST)
            dve.memset(m_sb[:, :], 0.0).then_inc(s_parts, 1)
            dve.tensor_copy(onehot[:, :], onehot_f[:, :]).then_inc(s_prep, 1)
            dve.tensor_tensor(shared[:, :, 0:HID], shared[:, :, 0:HID],
                              ident[:, :].rearrange("p (a n) -> p a n", a=1).broadcast_to((P, NLAY, P)), ALU.add).then_inc(s_route, 1)
            dve.wait_ge(s_route, 1)
            for l in range(NLAY):
                dve.tensor_tensor(experts[:, l, :, :], experts[:, l, :, :],
                                  shared[:, l, :].rearrange("p (a n) -> p a n", a=1).broadcast_to((P, NEXP + 1, HID + 1)), ALU.add).then_inc(s_prep, 1)
            dve.tensor_scalar(route_ok[:, :], route_i[:, :], 0.0, None, ALU.is_ge).then_inc(s_route, 1)
            dve.wait_ge(s_route, 2)
            dve.scalar_tensor_tensor(out=route_ok[:, :], in0=route_i[:, :], scalar=float(NEXP), in1=route_ok[:, :], op0=ALU.is_lt, op1=ALU.mult).then_inc(s_route, 1)
            dve.wait_ge(s_route, 3)
            dve.scalar_tensor_tensor(out=route_f[:, :], in0=route_i[:, :], scalar=-float(NEXP), in1=route_ok[:, :], op0=ALU.add, op1=ALU.mult).then_inc(s_parts, 1)
            dve.wait_ge(s_parts, 2)
            dve.tensor_scalar(route_x[:, :], route_f[:, :], float(NEXP), None, ALU.add).then_inc(s_route, 1)
            dve.tensor_copy(w_3[:, 0, :], w_bin[:, :]).then_inc(s_parts, 1)
            dve.wait_ge(s_parts, 3)
            dve.tensor_tensor(w_rest[:, :], w_bin[:, :], w_3[:, 0, :], ALU.subtract).then_inc(s_moved, 1)
            dve.wait_ge(s_moved, 1)
            dve.tensor_copy(w_3[:, 1, :], w_rest[:, :]).then_inc(s_parts, 1)
            dve.wait_ge(s_parts, 4)
            dve.tensor_tensor(w_3[:, 2, :], w_rest[:, :], w_3[:, 1, :], ALU.subtract).then_inc(s_parts, 1)
            dve.tensor_copy(pair_sel[:, :], pair_f[:, :]).then_inc(s_moved, 1)

            with dve.Fori(0, NT) as i:
                wait(dve, T1["qk_ps"], i + 1)
                wait(dve, T1["q_in"], i * 16 * NH)
                dve.tensor_tensor(t_cos[:, :], bank["J1"][:, :], cos[:, :], ALU.mult).then_inc(T1["rope_mul"], 1)
                dve.tensor_tensor(t_sin[:, :], bank["J2"][:, :], sin[:, :], ALU.mult).then_inc(T1["rope_mul"], 1)
                wait(dve, T1["rope_mul"], (i + 1) * 2)
                wait(dve, T1["scores"], i * TOKC["ng"])
                dve.tensor_tensor(rot[0:C, :], t_cos[0:C, :], t_sin[0:C, :], ALU.add).then_inc(T1["rope"], 1)
                for pc in range(2):
                    def half(b):
                        return b[C:2 * C, :].rearrange("k (n r p c) -> k p n r c", n=16, r=QP, p=2)[:, pc, :, :, :]
                    dve.tensor_tensor(rot[C:2 * C, :].rearrange("k (n p r c) -> k p n r c", n=16, r=QP, p=2)[:, pc, :, :, :],
                                      half(t_cos), half(t_sin), ALU.add).then_inc(T1["rope"], 1)
                attention(TOKC, i)
                wait(dve, T1["proj"], i + 1)
                dve.tensor_copy(rows(i * 4, 4), bank["J2"][:, 0:256].rearrange("p (t c) -> p t c", t=4)).then_inc(T1["h_done"], 1)
            wait(dve, T1["h_done"], NT)
            with dve.Fori(0, NT) as i:
                layer_norm(L, i, 4, row(i * 4), lambda t: xn[:, t, :])
                wait(dve, L["q_ps"], i + 1)
                wait(dve, L["stored"], i * 48)
                for t in range(2):
                    dve.tensor_scalar(q_sb[:, t * 256:(t + 1) * 256].rearrange("c (p r w) -> c p r w", p=16, r=QP),
                                      bank["J2"][0:C, t * 256:(t + 1) * 256].rearrange("c (r p w) -> c p r w", p=16, r=QP),
                                      temp[:, :], float(HD ** -0.5), ALU.mult, ALU.mult).then_inc(L["q_sb"], 1)
            with dve.Fori(0, NS) as i:
                attention(LOCC, i)
                wait(dve, T2["proj"], i + 1)
                dve.tensor_tensor(rows(i * 2, 2), bank["J2"][:, 0:128].rearrange("p (t c) -> p t c", t=2), rows(i * 2, 2), ALU.add).then_inc(T2["h_done"], 1)
            wait(dve, T2["h_done"], NS)
            with dve.Fori(0, NS) as i:
                layer_norm(FF, i, 2, row(i * 2), lambda t: xn[:, t, :])
                wait(dve, FF["out_ps"], i + 1)
                dve.tensor_tensor(rows(i * 2, 2), bank["AV"][:, 0:128].rearrange("p (t c) -> p t c", t=2), rows(i * 2, 2), ALU.add).then_inc(FF["h_done"], 1)
            wait(dve, FF["h_done"], NS)
            with dve.Fori(0, B) as b:
                wait(dve, RT["out_ps"], b * STRIPS)
                wait(dve, RT["state"], b * (2 * STRIPS))
                dve.memset(state[:, 0, :], 0.0).then_inc(RT["reset"], 1)
                wait(dve, RT["reset"], b + 1)
                settle(dve)
                with dve.Fori(0, STRIPS) as s:
                    i = b * STRIPS + s
                    layer_norm(RT, i, 2, row(i * 2), lambda t: xn[:, t, :])
                    wait(dve, RT["kv_ps"], i + 1)
                    dve.tensor_scalar(kd3[:, :, :], bank["J1"][:, 0:256].rearrange("p (t n) -> p t n", t=2)[:, :, 0:C],
                                      decay_k[:, :], None, ALU.mult).then_inc(RT["kd"], 1)
                    wait(dve, RT["qk_sb"], i + 1)
                    dve.tensor_tensor(qd3[:, :], qk3[:, 0:256], decay_q[:, :], ALU.mult).then_inc(RT["qd"], 1)
                    wait(dve, RT["s_ps"], i + 1)
                    dve.tensor_tensor(sd3[:, :, :], bank["MX"][:, 0:256].rearrange("p (t n) -> p t n", t=2),
                                      decay[:, :].rearrange("p (a n) -> p a n", a=1).broadcast_to((P, 2, P)), ALU.mult).then_inc(RT["sd"], 1)
                    for t in range(2):
                        wait(dve, RT["kv_sum"], i * 2 + t + 1)
                        wait(dve, RT["state"], i * 2 + t)
                        if t == 1:
                            wait(dve, RT["out_ps"], i + 1)
                        dve.scalar_tensor_tensor(out=state[:, 1 - t, :], in0=state[:, t, :], scalar=float(ALPHA ** P),
                                                 in1=bank["OT"][0:C, 0:C], op0=ALU.mult, op1=ALU.add).then_inc(RT["state"], 1)
                    dve.tensor_tensor(rows(i * 2, 2), bank["AV"][:, 0:128].rearrange("p (t c) -> p t c", t=2), rows(i * 2, 2), ALU.add).then_inc(RT["h_done"], 1)
            wait(dve, RT["h_done"], NS)
            with dve.Fori(0, NS) as i:
                layer_norm(BN, i, 2, row(i * 2), lambda t: xn2[:, t, :, :])
                wait(dve, BN["g_ps"], i + 1)
                dve.tensor_scalar(g3[:, :], bank["J1"][0:3 * NG, 0:256], 0.0, None, ALU.is_gt).then_inc(BN["gates"], 1)
                wait(dve, BN["xb"], i + 1)
                for k in range(8):
                    wait(dve, BN["sign"], i * 8 + k + 3)
                    wait(dve, BN["y_part"], i * 8 + k)
                    dve.tensor_tensor(prod[:, k % 2, :].rearrange("p (u n) -> p u n", u=4), sgn[:, k % 2, :].rearrange("p (u n) -> p u n", u=4),
                                      xb2[:, :].rearrange("p (a n) -> p a n", a=1).broadcast_to((P, 4, 256)), ALU.mult).then_inc(BN["prod"], 1)
                wait(dve, BN["y_part"], (i + 1) * 8)
                dve.tensor_tensor(ys[:, :, :], bank["AV"][:, 0:128].rearrange("p (t c) -> p t c", t=2),
                                  scale_bc[:, :].rearrange("p (a n) -> p a n", a=1).broadcast_to((P, 2, C)), ALU.mult).then_inc(BN["y_scaled"], 1)
                wait(dve, BN["y_scaled"], i + 1)
                wait(dve, BN["stored"], i * 16)
                dve.tensor_tensor(yo[:, :, :], ys[:, :, :], rows(i * 2, 2), ALU.add).then_inc(BN["y"], 1)


NLOADS = 31
NCONST = 11


def _with_bias(w, b):
    return np.concatenate([w, b[None, :]], 0)


def kernel(x, L0_tok_qkv_w, L0_tok_qkv_b, L0_tok_proj_w, L0_tok_proj_b, L0_attn_W_qkv, L0_attn_W_proj, L0_attn_b_proj,
           L0_attn_temperature, L0_ffn_route_id, L0_ffn_Wi, L0_ffn_bi, L0_ffn_Wr, L0_ffn_br, L0_ffn_Ws, L0_ffn_bs, L0_ffn_Wo,
           L0_ffn_bo, L1_attn_Wqkv, L1_attn_bqkv, L1_ffn_weight, L1_ffn_proj_w, L1_ffn_proj_b, L1_ffn_scale):
    import concourse.bacc as _bacc
    from concourse.bass_utils import run_bass_kernel_spmd as _run

    n = np.asarray
    arr = {k: v for k, v in shape_tables().items()}
    arr["pair"] = (np.arange(P)[:, None] // C == np.arange(2)[None, :]).astype(np.float32)
    arr["x"] = n(x)
    w, b = n(L0_tok_qkv_w), n(L0_tok_qkv_b)
    order = np.concatenate([np.arange(C) + C, np.arange(C)])
    arr["w_qk"] = _with_bias(w[order].T, b[order])
    arr["w_qk_swap"] = _with_bias(w[order ^ 1].T, b[order ^ 1])
    arr["w_v1"] = _with_bias(w[2 * C:].T, b[2 * C:])
    arr["w_p1"] = _with_bias(n(L0_tok_proj_w).T, n(L0_tok_proj_b))
    w = n(L0_attn_W_qkv)
    arr["w_q2"], arr["w_k2"], arr["w_v2"] = w[:C].T, w[C:2 * C].T, w[2 * C:].T
    arr["w_p2"] = _with_bias(n(L0_attn_W_proj).T, n(L0_attn_b_proj))
    arr["temp"] = n(L0_attn_temperature).reshape(1, 1)
    arr["w_i"] = _with_bias(n(L0_ffn_Wi).T, n(L0_ffn_bi))
    wr, br, ws, bs = n(L0_ffn_Wr), n(L0_ffn_br), n(L0_ffn_Ws), n(L0_ffn_bs)
    arr["experts"] = np.concatenate([wr.transpose(3, 0, 1, 2), br.transpose(2, 0, 1)[..., None]], 3)
    arr["shared"] = np.concatenate([ws[:, 0].transpose(2, 0, 1), bs[:, 0].T[..., None]], 2)
    arr["w_o"], arr["b_o"] = n(L0_ffn_Wo).T, n(L0_ffn_bo).reshape(1, C)
    arr["route"] = n(L0_ffn_route_id).reshape(1, -1)
    w, b = n(L1_attn_Wqkv), n(L1_attn_bqkv)
    arr["w_q3"], arr["w_k3"] = _with_bias(w[:, :C], b[:C]), _with_bias(w[:, C:2 * C], b[C:2 * C])
    arr["w_kv3"] = _with_bias(w[:, C:], b[C:])
    g = _with_bias(n(L1_ffn_proj_w).T, n(L1_ffn_proj_b))
    arr["w_gate"] = np.concatenate([g, g, g], 1)
    arr["w_bin"] = n(L1_ffn_weight)[0].reshape(NG, C, C // 2, 2).transpose(0, 2, 3, 1).reshape(P, -1)
    arr["scale"] = n(L1_ffn_scale).reshape(1, C)

    nc = _bacc.Bacc("TRN2", target_bir_lowering=False, num_devices=1)
    arrays, aps = {}, {}
    for k, v in arr.items():
        v = np.ascontiguousarray(v)
        arrays["in_" + k] = v
        aps[k] = nc.dram_tensor("in_" + k, v.shape, mybir.dt.from_np(v.dtype), kind="ExternalInput").ap()
    o = nc.dram_tensor("out_0", (B, H * W, C), F32, kind="ExternalOutput").ap()
    build(nc, aps, o)
    return _run(nc, [arrays], core_ids=[0]).results[0]["out_0"]
```

```python
from contextlib import ExitStack

import numpy as np
import concourse.bass as bass
from concourse import mybir

F32 = mybir.dt.float32
BF16 = mybir.dt.bfloat16
I32 = mybir.dt.int32
ALU = mybir.AluOpType
ACT = mybir.ActivationFunctionType
AX = mybir.AxisListType

P = 128
B, H, W, C = 4, 64, 64, 64
NH, HD = 8, 8
TOK = B * H * W
TILES = TOK // P
WIN = 8
QP = 4
NQ = QP * QP
HALF = 3
KS = QP + 2 * HALF
NKL = KS * KS
NKT = WIN * WIN
PW = W + 2 * HALF
CMOD = 12
NAUG = KS + CMOD + 1
BIG = 1.0e9
HID, NEXP, NLAY = 128, 16, 2
KL_ROWS = C + NAUG
NG = 8
EPS = 1e-5
ALPHA = 0.99
STRIPS = H // QP
GP = 4


def shape_tables():
    t = {}
    t["ident"] = np.eye(P, dtype=np.float32)
    ch = np.arange(C)
    d = ch % HD
    half = HD // 2
    freq = (1.0 / 10000.0 ** (np.arange(0, half, 2, dtype=np.float32) / half)).astype(np.float32)
    f = freq[(d % half) // 2]
    wpos = np.arange(WIN * W)
    pos = np.where((d < half)[:, None], (wpos // WIN % WIN)[None, :], (wpos % WIN)[None, :])
    ang = (pos.astype(np.float32) * f[:, None]).astype(np.float32)
    cos, sin = np.cos(ang), np.sin(ang) * np.where(d % 2 == 0, -1.0, 1.0)[:, None]
    scale = np.float32(HD ** -0.5)
    t["cos"] = np.concatenate([cos, cos * scale]).astype(np.float32)
    t["sin"] = np.concatenate([sin, sin * scale]).astype(np.float32)
    hq = np.arange(P)
    t["headmask"] = (hq[:, None] // NQ == ch[None, :] // HD).astype(np.float32)
    t["sel"] = (hq[:, None] % NQ == np.arange(NQ)[None, :]).astype(np.float32)
    t["onehot"] = np.repeat(np.eye(32, dtype=np.float32)[:, :, None], NKL, 2).reshape(32, -1)
    aug = np.zeros((STRIPS, NAUG, KS, PW), np.float32)
    for r in range(KS):
        aug[:, r, r, :] = 1
    for c in range(PW):
        aug[:, KS + c % CMOD, :, c] = 1
        if c < HALF or c >= PW - HALF:
            aug[:, KS + CMOD, :, c] = 1
    aug[0, KS + CMOD, :HALF, :] = 1
    aug[STRIPS - 1, KS + CMOD, KS - HALF:, :] = 1
    t["kaug"] = aug.reshape(STRIPS, NAUG, KS * PW)
    qa = np.zeros((NAUG, QP, W), np.float32)
    for r in range(QP):
        for kr in range(KS):
            if abs(kr - HALF - r) > HALF:
                qa[kr, r, :] = -BIG
    for c in range(W):
        j = c // QP
        for kc in range(KS):
            if abs(kc - HALF - c % QP) > HALF:
                qa[KS + (QP * j + kc) % CMOD, :, c] = -BIG
    qa[KS + CMOD] = -BIG
    qa = qa.reshape(NAUG, QP, W // QP, QP).transpose(0, 2, 1, 3).reshape(NAUG, W // QP, 1, NQ)
    t["qaug"] = np.repeat(qa, NH, 2).reshape(NAUG, -1)
    i = np.arange(P, dtype=np.float64)
    dm = np.where(i[None, :] >= i[:, None], ALPHA ** (i[None, :] - i[:, None]), 0.0) / np.sqrt(C)
    t["decay"] = dm.astype(np.float32)
    t["decay_q"] = np.tile((ALPHA ** (i + 1) / np.sqrt(C))[None, :], (C, 2)).astype(np.float32)
    t["keep"] = np.repeat((np.arange(TOK // 256) % STRIPS != 0).astype(np.float32)[None, :], P, 0)
    t["decay_k"] = (ALPHA ** (P - 1 - i))[:, None].astype(np.float32)
    return t


def build(nc, a, out):
    ctx = ExitStack()
    with ctx:
        def sb(name, shape, dt=F32):
            return ctx.enter_context(nc.sbuf_tensor(name, shape, dt))

        def sem(name):
            return ctx.enter_context(nc.semaphore(name))

        bank = {n: ctx.enter_context(nc.psum_tensor("ps_" + n, [P, 512], F32)) for n in ("T", "J1", "AV", "OT")}
        double = [ctx.enter_context(nc.psum_tensor("ps_D%d" % n, [P, 1024], F32)) for n in range(2)]
        bank["J2"], bank["MX"] = double[0][:, 0:512], double[0][:, 512:1024]
        bank["S0"], bank["S1"] = double[1][:, 0:512], double[1][:, 512:1024]

        h = sb("h", [P, TILES, C])
        ident = sb("ident", [P, P])
        cos, sin = sb("cos", [P, 512]), sb("sin", [P, 512])
        headmask, sel = sb("headmask", [P, C]), sb("sel", [P, NQ])
        onehot_f, onehot = sb("onehot_f", [32, 32 * NKL]), sb("onehot", [P, 32 * NKL], BF16)
        decay, decay_q, decay_k = sb("decay", [P, P]), sb("decay_q", [C, 256]), sb("decay_k", [P, 1])
        w_qk, w_qk_swap, w_v1, w_p1 = sb("w_qk", [P, 128]), sb("w_qk_swap", [P, 128]), sb("w_v1", [P, C]), sb("w_p1", [P, C])
        w_q2, w_k2, w_v2, w_p2 = sb("w_q2", [P, C]), sb("w_k2", [P, C]), sb("w_v2", [P, C]), sb("w_p2", [P, C])
        temp = sb("temp", [C, 1])
        w_i = sb("w_i", [P, HID])
        experts = sb("experts", [P, NLAY, NEXP + 1, HID + 1])
        shared = sb("shared", [P, NLAY, HID + 1])
        w_o, b_o, ones_row = sb("w_o", [P, C]), sb("b_o", [P, C]), sb("ones_row", [P, P])
        w_q3, w_k3, w_kv3 = sb("w_q3", [P, C]), sb("w_k3", [P, C]), sb("w_kv3", [P, 128])
        w_gate = sb("w_gate", [P, 3 * NG])
        w_bin, w_rest = sb("w_bin", [P, C * C * NG // P]), sb("w_rest", [P, C * C * NG // P])
        w_3 = sb("w_3", [P, 3, C * C * NG // P], BF16)
        w_parts = sb("w_parts", [P, C * C], BF16)
        pair_sel = sb("pair_sel", [P, 2], BF16)
        pair_f = sb("pair_f", [P, 2])
        scale_bc = sb("scale_bc", [P, C])
        route_i, route_f, route_ok, route_x = sb("route_i", [1, 64], I32), sb("route_f", [1, 64]), sb("route_ok", [1, 64]), sb("route_x", [1, 64], I32)
        minus_half = sb("minus_half", [P, 4])
        zeros = sb("zeros", [C, HALF * PW])

        xin = sb("xin", [P, 4, C])
        xT = sb("xT", [P, 512])
        t_cos, t_sin, rot = sb("t_cos", [P, 512]), sb("t_sin", [P, 512]), sb("rot", [P, 512])
        qexp = sb("qexp", [P, NH * 512])
        q_blocks = qexp[:, :].rearrange("k (p h q) -> k p h q", h=NH, q=NQ)
        kpatch, xpatch = sb("kpatch", [P, 16 * NKL]), sb("xpatch", [P, 16 * NKL])
        kst, xst = sb("kst", [P, KS * PW]), sb("xst", [C, KS * PW])
        vsb = sb("vsb", [P, 16, P])
        m_sb, mT = sb("m_sb", [P, P]), sb("mT", [P, P], BF16)
        prob = sb("prob", [P, 2, 512])
        rec, selr, msk = sb("rec", [P, 2, GP]), sb("selr", [P, 2, GP * NQ]), sb("msk", [P, 2, GP * C])
        aT = sb("aT", [P, 512])
        rstd_warm = sb("table_warm", [P, 1])
        xn = sb("xn", [P, 4, C])
        xpad, kpad, q_sb = sb("xpad", [P, WIN * PW]), sb("kpad", [C, WIN * PW]), sb("q_sb", [C, 512])
        xnT = [sb("xnT%d" % n, [P, 256]) for n in range(3)]
        ln_sb = {}
        for n, t in (("pre", 4), ("ffn", 2), ("ret", 2), ("bin", 2)):
            ln_sb[n] = (sb("stats_" + n, [P, t, 6]), sb("mv_" + n, [P, t, 2]), sb("veps_" + n, [P, t]), sb("rstd_" + n, [P, t]))
        xn_f, xn_r = sb("xn_f", [P, 2, C]), sb("xn_r", [P, 2, C])
        keep = sb("keep", [P, NSTRIP])
        hidT = sb("hidT", [P, 3, 256])
        w_exp = sb("w_exp", [P, NLAY, HID + 1])
        qk3, qd3 = sb("qk3", [P, 512]), sb("qd3", [P, 256])
        kd3, v3, sd3 = sb("kd3", [P, 2, C]), sb("v3", [P, 2, C]), sb("sd3", [P, 2, P])
        state = sb("state", [P, 2, C])
        xn2 = sb("xn2", [P, 2, 2, C])
        xb2 = sb("xb2", [P, 2, 256], BF16)
        g3 = sb("g3", [P, 2, 256], BF16)
        sgn, prod = sb("sgn", [P, 2, 1024], BF16), sb("prod", [P, 2, 1024], BF16)
        ys, yo = sb("ys", [P, 2, C]), sb("yo", [P, 2, C])

        kx_d = nc.dram_tensor("kx_d", (B, 2, C, PW * PW), F32, kind="Internal").ap()
        qs_d = nc.dram_tensor("qs_d", (C, TOK), F32, kind="Internal").ap()
        x_v = a["x"].rearrange("b (t y) w c -> (y w) (b t) c", y=2)
        o_v = out.rearrange("b (t p) c -> p (b t) c", p=P)

        s_w = sem("weights_loaded")
        s_const = sem("constants_made")
        s_prep = sem("experts_combined")
        s_route = sem("routes_ready")
        s_parts = sem("gate_weights_split")
        s_moved = sem("gate_weight_parts_moved")

        def named(prefix, *names):
            return {n: sem(prefix + "_" + n) for n in names}

        def wait(eng, semaphore, count, most=None):
            if isinstance(count, int):
                count = min(count, most) if most else count
                if count <= 0:
                    return
            eng.wait_ge(semaphore, count + 1)

        s_settled = sem("settled")

        def settle(eng):
            eng.sem_inc(s_settled, 1)

        core = ("max_scores", "max_done", "maxT", "negmax", "scores", "exp_done", "av_done", "rec_done",
                "norm_done", "sel_done", "attn_out", "v_ps", "v_sb", "q_in", "k_in", "x_patch", "k_patch", "proj", "h_done")
        T1 = named("tok", "x_in", "xT_ps", "xT_sb", "qk_ps", "rope_mul", "rope", *core)
        T2 = named("loc", *core)
        L = named("pre", "stats", "mv", "veps", "rstd", "xn", "xT_ps", "xT_sb", "k_ps", "q_ps", "k_sb", "q_sb", "stored", "padded")
        FF = named("ffn", "stats", "mv", "veps", "rstd", "xn", "xT_ps", "xT_sb", "w_in", "hid_ps", "hid_sb", "out_ps", "h_done")
        RT = named("ret", "stats", "mv", "veps", "rstd", "xn", "xT_ps", "xT_sb", "qk_ps", "qk_sb", "kv_ps", "kd", "v", "qd", "s_ps",
                   "sd", "kv_sum", "state", "reset", "out_ps", "h_done")
        BN = named("bin", "stats", "mv", "veps", "rstd", "xn", "xT_ps", "xb", "xT_sb", "g_ps", "gates", "w_ps", "sign", "prod",
                   "y_part", "y_ps", "y_scaled", "y", "stored")

        def cfg(s, nk, kdim, rows, keys, qview, vkeys, npatch):
            return dict(s=s, nk=nk, kdim=kdim, rows=rows, keys=keys, q=qview, v=vkeys, np=npatch, ng=npatch // GP)

        KL = C + NAUG

        def operands(q, k, nk):
            def of(buf, n, at, narrow):
                if narrow:
                    return buf[:, at * n:(at + 1) * n].bitcast(BF16).rearrange("p (n e) -> p n e", e=2)[:, :, 1]
                return buf[:, at * n:(at + 1) * n]
            return (lambda p, narrow: of(q, P, p, narrow)), (lambda p, narrow: of(k, nk, NKEY[nk](p), narrow))

        NKEY = {NKT: lambda p: p // 4, NKL: lambda p: p}
        tok_q, tok_k = operands(qexp, rot, NKT)
        loc_q, loc_k = operands(qexp, kpatch, NKL)

        def tok_at(p):
            return QP * (p // 2 % 2), WIN * (p // 4) + QP * (p % 2)

        def loc_at(p):
            return 0, QP * p

        TOKC = dict(nv=1, s=T1, nk=NKT, np=32, ng=8, q=tok_q, k=tok_k, kv=P, v=lambda p: vsb[:, p // 4, :], at=tok_at)
        LOCC = dict(nv=2, s=T2, nk=NKL, np=16, ng=4, q=loc_q, k=loc_k, kv=NKL, v=lambda p: vsb[0:NKL, p, :], at=loc_at)
        onehot_v = onehot[:, :].rearrange("k (p n) -> k p n", p=32)
        S = [bank["S0"], bank["S1"]]

        def inside(i):
            return i if not isinstance(i, int) or 0 <= i < NSTRIP else None

        def staggered(eng, strips):
            for j in range(3):
                strips(j, j % 2)
            with eng.Fori(3, NSTRIP - 1, 2) as j:
                strips(j, 1)
                strips(j + 1, 0)
            for j in range(NSTRIP - 1, NSTRIP + 3):
                strips(j, j % 2)

        NT = TOK // 512
        NS = TOK // 256

        block = ctx.enter_context(nc.Block())

        @block.sync
        def _(sp):
            loads = [(ident[:, :], a["ident"]), (cos[:, :], a["cos"]), (sin[:, :], a["sin"]), (headmask[:, :], a["headmask"]),
                     (sel[:, :], a["sel"]), (onehot_f[:, :], a["onehot"]), (decay[:, :], a["decay"]), (decay_q[:, :], a["decay_q"]),
                     (decay_k[:, :], a["decay_k"]), (w_qk[:, :], a["w_qk"]), (w_qk_swap[:, :], a["w_qk_swap"]), (w_v1[:, :], a["w_v1"]),
                     (w_p1[:, :], a["w_p1"]), (w_q2[:, :], a["w_q2"]), (w_k2[:, :], a["w_k2"]), (w_v2[:, :], a["w_v2"]),
                     (w_p2[:, :], a["w_p2"]), (temp[:, :], a["temp"].broadcast_to((C, 1))), (w_i[:, :], a["w_i"]),
                     (shared[:, :, :], a["shared"]), (w_o[:, :], a["w_o"]), (b_o[:, :], a["b_o"]),
                     (w_q3[:, :], a["w_q3"]), (w_k3[:, :], a["w_k3"]), (w_kv3[:, :], a["w_kv3"]), (w_gate[:, :], a["w_gate"]),
                     (w_bin[:, :], a["w_bin"]), (pair_f[:, :], a["pair"]), (scale_bc[:, :], a["scale"].broadcast_to((P, C))),
                     (route_i[:, :], a["route"]), (keep[:, :], a["keep"]), (experts[:, :, 0:NEXP, :], a["experts"])]
            for stage in (T1, T2, L, FF, RT, BN):
                for signal in stage.values():
                    sp.sem_inc(signal, 1)
            for dst, src in loads:
                sp.dma_start(dst, src).then_inc(s_w, 16)
            assert len(loads) == NLOADS
            with sp.Fori(0, NT) as i:
                wait(sp, T1["xT_ps"], i)
                sp.dma_start(xin[:, :, :], x_v[:, bass.ds(i * 4, 4), :]).then_inc(T1["x_in"], 16)
                wait(sp, T1["rope"], (i + 1) * 3)
                wait(sp, T1["scores"], i * TOKC["ng"])
                for n in range(NH):
                    sp.dma_start(q_blocks[n * HD:(n + 1) * HD, :, n, :],
                                 rot[C + n * HD:C + (n + 1) * HD, :].rearrange("d (p q) -> d p q", q=NQ)).then_inc(T1["q_in"], 16)
            sp.wait_ge(s_const, NCONST)
            for b in range(B):
                for j in range(2):
                    for at in (0, (PW - HALF) * PW):
                        sp.dma_start(kx_d[b, j, :, at:at + HALF * PW], zeros[:, :]).then_inc(L["padded"], 16)
            with sp.Fori(0, B) as b:
                with sp.Fori(0, WIN) as w:
                    i = b * WIN + w
                    dst = kx_d.rearrange("b j c n -> (b j) c n")
                    wait(sp, L["xT_sb"], i + 1 + 1)
                    settle(sp)
                    wait(sp, L["k_sb"], i + 1)
                    settle(sp)
                    wait(sp, L["q_sb"], (i + 1) * 2)
                    settle(sp)
                    sp.dma_start(dst[bass.ds(b * 2 + 1, 1), :, bass.ds((w * WIN + HALF) * PW, WIN * PW)].rearrange("a c n -> (a c) n"),
                                 xpad[0:C, :]).then_inc(L["stored"], 16)
                    sp.dma_start(dst[bass.ds(b * 2, 1), :, bass.ds((w * WIN + HALF) * PW, WIN * PW)].rearrange("a c n -> (a c) n"),
                                 kpad[:, :]).then_inc(L["stored"], 16)
                    sp.dma_start(qs_d[:, bass.ds(i * 512, 512)], q_sb[:, :]).then_inc(L["stored"], 16)
            wait(sp, L["stored"], 48 * NT)
            wait(sp, L["padded"], 16 * 4 * B)
            wait(sp, T1["scores"], NT * TOKC["ng"])
            sp.dma_start(qexp[C:KL, 0:NH * 256], a["qaug"]).then_inc(T2["q_in"], 16)
            with sp.Fori(0, B) as b:
                with sp.Fori(0, STRIPS) as s:
                    i = b * STRIPS + s
                    src = kx_d.rearrange("b j c n -> (b j) c n")
                    wait(sp, T2["x_patch"], i)
                    settle(sp)
                    sp.dma_start(xst[:, :], src[bass.ds(b * 2 + 1, 1), :, bass.ds(s * (QP * PW), KS * PW)].rearrange("a c n -> (a c) n")).then_inc(T2["k_in"], 16)
                    wait(sp, T2["k_patch"], i)
                    settle(sp)
                    sp.dma_start(kst[0:C, :], src[bass.ds(b * 2, 1), :, bass.ds(s * (QP * PW), KS * PW)].rearrange("a c n -> (a c) n")).then_inc(T2["k_in"], 16)
                    sp.dma_start(kst[C:KL, :], a["kaug"][bass.ds(s, 1), :, :].rearrange("a c n -> (a c) n")).then_inc(T2["k_in"], 16)
                    wait(sp, T2["scores"], i * LOCC["ng"])
                    for n in range(NH):
                        sp.dma_start(q_blocks[n * HD:(n + 1) * HD, 0:16, n, :],
                                     qs_d[n * HD:(n + 1) * HD, bass.ds(i * 256, 256)].rearrange("d (p q) -> d p q", q=NQ)).then_inc(T2["q_in"], 16)
            sp.wait_ge(s_prep, 2)
            sp.wait_ge(s_route, 4)
            sp.wait_ge(s_parts, 5)
            for k in range(3):
                for g in range(NG):
                    r = P // NG
                    sp.dma_start(w_parts[k * NG + g:k * NG + g + 1, :].rearrange("a (r n) -> a r n", r=r), w_3[g * r:(g + 1) * r, k:k + 1, :]).then_inc(s_moved, 16)

            def weights_in(i):
                wait(sp, FF["hid_sb"], i * 3)
                settle(sp)
                e = sp.value_load(route_x[0:1, bass.ds(i, 1)], min_val=0, max_val=NEXP)
                sp.dma_start(w_exp[:, :, :], experts[:, :, bass.ds(e, 1), :].rearrange("p l a n -> p l (a n)")).then_inc(FF["w_in"], 16)

            def store(i):
                wait(sp, BN["y"], i + 1)
                settle(sp)
                sp.dma_start(o_v[:, bass.ds(i * 2, 2), :], yo[:, :, :]).then_inc(BN["stored"], 16)

            def stores(j):
                if not isinstance(j, int) or j < NS:
                    weights_in(j)
                if not isinstance(j, int) or j >= 4:
                    store(j - 4)

            for j in range(4):
                stores(j)
            with sp.Fori(4, NS) as j:
                stores(j)
            for j in range(NS, NS + 4):
                stores(j)
            wait(sp, BN["stored"], 16 * NS)

        @block.gpsimd
        def _(gp):
            fills = [(xT[:, :], 0.0), (aT[:, :], 0.0), (xnT[0][:, :], 0.0), (xnT[1][:, :], 0.0), (xnT[2][:, :], 0.0), (xT[C:C + 1, :], 1.0), (aT[C:C + 1, :], 1.0), (xnT[0][C:C + 1, :], 1.0), (xnT[1][C:C + 1, :], 1.0), (xnT[2][C:C + 1, :], 1.0),
                     (ones_row[:, :], 0.0), (ones_row[0:1, :], 1.0), (minus_half[:, :], -0.5), (zeros[:, :], 0.0), (xpad[:, :], 0.0),
                     (kpad[:, :], 0.0), (vsb[:, :, :], 0.0), (vsb[:, :, C:C + 1], 1.0), (qexp[:, :], 0.0), (onehot[:, :], 0.0),
                     (kpatch[:, :], 0.0), (xpatch[:, :], 0.0), (prob[:, :, :], 0.0), (qk3[:, :], 0.0), (qd3[:, :], 0.0), (state[:, :, :], 0.0),
                     (g3[:, :, :], 0.0), (w_parts[:, :], 0.0), (m_sb[:, :], 0.0), (experts[:, :, NEXP:NEXP + 1, :], 0.0)]
            assert len(fills) == NCONST
            for n, (dst, value) in enumerate(fills):
                if n:
                    gp.wait_ge(s_const, n)
                gp.memset(dst, value).then_inc(s_const, 1)
            gp.wait_ge(s_const, NCONST)
            def patches(buf, n):
                v = buf[0:n, :]
                return bass.AP(v.tensor, v.offset, [list(v.ap[0]), [QP, 16], [PW, KS], [1, KS]])

            def inv_std(name, q, i, after):
                _, _, veps, rstd = ln_sb[name]
                wait(gp, *after)
                wait(gp, q["veps"], i + 1)
                gp.tensor_tensor(rstd[:, :], veps[:, :], minus_half[:, 0:veps.shape[1]], ALU.pow).then_inc(q["rstd"], 1)

            with gp.Fori(0, NT) as i:
                inv_std("pre", L, i, (L["rstd"], i))
            with gp.Fori(0, NS) as i:
                wait(gp, T2["k_in"], (i + 1) * 48)
                wait(gp, T2["k_patch"], i)
                wait(gp, T2["v_ps"], i * 2)
                settle(gp)
                gp.tensor_copy(xpatch[0:C, :].rearrange("c (p r w) -> c p r w", p=16, r=KS), patches(xst, C)).then_inc(T2["x_patch"], 1)
                wait(gp, T2["scores"], i * LOCC["ng"])
                settle(gp)
                wait(gp, T2["x_patch"], i + 1)
                settle(gp)
                gp.tensor_copy(kpatch[0:KL, :].rearrange("c (p r w) -> c p r w", p=16, r=KS), patches(kst, KL)).then_inc(T2["k_patch"], 1)

            def inv_stds(j):
                if not isinstance(j, int) or j < NS:
                    inv_std("ffn", FF, j, (BN["rstd"], j - 2))
                if not isinstance(j, int) or 1 <= j < NS + 1:
                    inv_std("ret", RT, j - 1, (FF["rstd"], j + 1, NS))
                if not isinstance(j, int) or j >= 2:
                    inv_std("bin", BN, j - 2, (RT["rstd"], j, NS))

            for j in range(2):
                inv_stds(j)
            with gp.Fori(2, NS) as j:
                inv_stds(j)
            for j in range(NS, NS + 2):
                inv_stds(j)

        @block.tensor
        def _(pe):
            def attention(c, i):
                q, nk, ng = c["s"], c["nk"], c["ng"]
                for g in range(ng):
                    wait(pe, q["max_done"], i * ng + g)
                    for u in range(GP):
                        mm = pe.matmul(bank["MX"][:, u * nk:(u + 1) * nk], c["q"](g * GP + u, True), c["k"](g * GP + u, True),
                                       start=True, stop=True)
                    mm.then_inc(q["max_scores"], 1)
                wait(pe, q["max_done"], (i + 1) * ng)
                pe.transpose(bank["T"][:, 0:P], m_sb[:, :], ident[:, :]).then_inc(q["maxT"], 1)
                wait(pe, q["negmax"], i + 1)

                def scores(g):
                    wait(pe, q["exp_done"], i * ng + g + 1)
                    settle(pe)
                    for u in range(GP):
                        o = S[g % 2][0:nk, u * P:(u + 1) * P]
                        pe.matmul(o, c["k"](g * GP + u, False), c["q"](g * GP + u, False), start=True, stop=False)
                        mm = pe.matmul(o, onehot_v[:, g * GP + u, 0:nk], mT[:, :], start=False, stop=True)
                    mm.then_inc(q["scores"], 1)

                def values(g):
                    wait(pe, q["exp_done"], i * ng + g + 3)
                    wait(pe, q["norm_done"], (i * ng + g) * 2)
                    for u in range(GP):
                        mm = pe.matmul(bank["AV"][:, u * P:(u + 1) * P], prob[0:c["kv"], g % 2, u * P:(u + 1) * P],
                                       c["v"](g * GP + u), start=True, stop=True)
                    mm.then_inc(q["av_done"], 1)

                def select(g):
                    wait(pe, q["norm_done"], (i * ng + g + 1) * 2)
                    for u in range(GP):
                        p = g * GP + u
                        r, w = c["at"](p)
                        o = bank["OT"][0:C, :].rearrange("c (r w) -> c r w", w=W)[:, r:r + QP, w:w + QP]
                        mm = pe.matmul(o, msk[:, g % 2, u * C:(u + 1) * C], selr[:, g % 2, u * NQ:(u + 1) * NQ], start=True, stop=True)
                    mm.then_inc(q["sel_done"], 1)

                for g in range(ng + 2):
                    if g < ng:
                        scores(g)
                    if 1 <= g <= ng:
                        if g == 1:
                            wait(pe, q["v_sb"], (i + 1) * c["nv"])
                        values(g - 1)
                    if g >= 2:
                        select(g - 2)

            def project(q, i, n, w):
                wait(pe, q["attn_out"], i + 1)
                wait(pe, q["h_done"], i)
                for t in range(n):
                    mm = pe.matmul(bank["J2"][:, t * C:(t + 1) * C], aT[:, t * P:(t + 1) * P], w[:, :], start=True, stop=True)
                mm.then_inc(q["proj"], 1)

            def turn(src, width, n, q, k):
                settle(pe)
                for t in range(n):
                    mm = pe.transpose(bank["T"][0:width, t * P:(t + 1) * P], src(t), ident[:, :])
                mm.then_inc(q[k], 1)

            pe.wait_ge(s_w, 16 * NLOADS)
            pe.wait_ge(s_const, NCONST)
            pe.wait_ge(s_prep, 3)
            with pe.Fori(0, NT) as i:
                wait(pe, T1["x_in"], (i + 1) * 16)
                wait(pe, T1["negmax"], i)
                turn(lambda t: xin[:, t, :], C, 4, T1, "xT_ps")
                wait(pe, T1["xT_sb"], i + 1)
                wait(pe, T1["h_done"], i)
                pe.matmul(bank["J1"][:, :], w_qk[:, :], xT[:, :], start=True, stop=True)
                pe.matmul(bank["J2"][:, :], w_qk_swap[:, :], xT[:, :], start=True, stop=True).then_inc(T1["qk_ps"], 1)
                wait(pe, T1["attn_out"], i)
                for n in range(8):
                    mm = pe.matmul(bank["OT"][0:NKT, n * C:(n + 1) * C], xT[:, n * NKT:(n + 1) * NKT], w_v1[:, :], start=True, stop=True)
                mm.then_inc(T1["v_ps"], 1)
                wait(pe, T1["v_sb"], i + 1)
                wait(pe, T1["q_in"], (i + 1) * 16 * NH)
                wait(pe, T1["rope"], (i + 1) * 3)
                attention(TOKC, i)
                project(T1, i, 4, w_p1)
            with pe.Fori(0, NT) as i:
                wait(pe, L["xn"], (i + 1) * 4)
                turn(lambda t: xn[:, t, :], C, 4, L, "xT_ps")
                wait(pe, L["xT_sb"], i + 2)
                wait(pe, L["k_sb"], i)
                wait(pe, L["q_sb"], i * 2)
                xw = xpad[:, :].rearrange("c (r w) -> c r w", w=PW)[:, :, HALF:HALF + W]
                settle(pe)
                pe.matmul(bank["J1"][0:C, :], w_k2[:, :], xw, start=True, stop=True).then_inc(L["k_ps"], 1)
                pe.matmul(bank["J2"][0:C, :], w_q2[:, :], xw, start=True, stop=True).then_inc(L["q_ps"], 1)
            with pe.Fori(0, NS) as i:
                wait(pe, T2["x_patch"], i + 1)
                wait(pe, T2["k_patch"], i + 1)
                wait(pe, T2["q_in"], (i + 1) * 16 * NH + 16)
                for hf in range(2):
                    if hf == 0:
                        wait(pe, T2["attn_out"], i)
                    else:
                        wait(pe, T2["v_sb"], i * 2 + 1)
                    for u in range(8):
                        p = hf * 8 + u
                        mm = pe.matmul(bank["OT"][0:NKL, u * C:(u + 1) * C], xpatch[:, p * NKL:(p + 1) * NKL], w_v2[:, :], start=True, stop=True)
                    mm.then_inc(T2["v_ps"], 1)
                wait(pe, T2["v_sb"], i * 2 + 2)
                attention(LOCC, i)
                project(T2, i, 2, w_p2)
            pe.wait_ge(s_moved, 16 * 3 * NG + 2)

            def strips(j, par):
                f, r, g, q = (inside(j - k) for k in range(4))

                def weights(q, k, half):
                    wait(pe, BN["sign"], q * 8 + k + 1)
                    for u in range(4):
                        mm = pe.matmul(double[k % 2][:, u * 256:(u + 1) * 256],
                                       w_parts[:, (k * 4 + u) * P:(k * 4 + u + 1) * P], g3[:, half, :], start=True, stop=True)
                    mm.then_inc(BN["w_ps"], 1)

                def reduce(k):
                    if k == 0:
                        wait(pe, BN["y_scaled"], q)
                    wait(pe, BN["prod"], q * 8 + k + 1)
                    for u in range(4):
                        for t in range(2):
                            mm = pe.matmul(bank["AV"][:, t * C + (k * 4 + u) * 2:t * C + (k * 4 + u) * 2 + 2],
                                           prod[:, k % 2, u * 256 + t * P:u * 256 + (t + 1) * P], pair_sel[:, :], start=True, stop=True)
                    mm.then_inc(BN["y_part"], 1)

                for k in range(8):
                    if k < 7 and q is not None:
                        weights(q, k + 1, 1 - par)
                    if k == 7 and g is not None:
                        wait(pe, BN["gates"], g + 1)
                        weights(g, 0, par)
                    if k and q is not None:
                        reduce(k - 1)
                    if k == 0 and f is not None:
                        wait(pe, FF["xn"], (f + 1) * 2)
                        wait(pe, RT["state"], (f - 1) * 2, 2 * NS)
                        turn(lambda t: xn_f[:, t, :], C, 2, FF, "xT_ps")
                    if k == 1:
                        if f is not None:
                            wait(pe, FF["xT_sb"], f + 1)
                            wait(pe, FF["h_done"], f)
                            pe.matmul(bank["J1"][:, 0:256], w_i[:, :], xnT[0][:, :], start=True, stop=True).then_inc(FF["hid_ps"], 1)
                        if r is not None:
                            wait(pe, RT["xn"], (r + 1) * 2)
                            wait(pe, FF["xT_sb"], r + 2, NS)
                            turn(lambda t: xn_r[:, t, :], C, 2, RT, "xT_ps")
                    if k == 2:
                        if f is not None:
                            wait(pe, FF["w_in"], (f + 1) * 16)
                            wait(pe, FF["hid_sb"], f * 3 + 1)
                            pe.matmul(bank["J1"][:, 0:256], w_exp[:, 0, 0:HID], hidT[:, 0, :], start=True, stop=True).then_inc(FF["hid_ps"], 1)
                        if g is not None:
                            wait(pe, BN["xn"], (g + 1) * 2)
                            wait(pe, RT["xT_sb"], g + 2, NS)
                            turn(lambda t: xn2[:, t, :, :], P, 2, BN, "xT_ps")
                        if r is not None:
                            wait(pe, RT["xT_sb"], r + 1)
                            wait(pe, RT["h_done"], r)
                            settle(pe)
                            pe.matmul(bank["OT"][0:C, 0:256], w_q3[:, :], xnT[1][:, :], start=True, stop=True)
                            pe.matmul(bank["OT"][0:C, 256:512], w_k3[:, :], xnT[1][:, :], start=True, stop=True).then_inc(RT["qk_ps"], 1)
                    if k == 3:
                        if g is not None:
                            wait(pe, BN["xT_sb"], g + 1)
                            wait(pe, FF["hid_sb"], g * 3 + 8, 3 * NS)
                            settle(pe)
                            pe.matmul(bank["J1"][0:3 * NG, 0:256], w_gate[:, :], xnT[2][:, :], start=True, stop=True).then_inc(BN["g_ps"], 1)
                        if r is not None:
                            wait(pe, BN["xb"], r)
                            wait(pe, BN["xT_sb"], r)
                            for t in range(2):
                                mm = pe.matmul(bank["T"][:, t * P:(t + 1) * P], xnT[1][:, t * P:(t + 1) * P], w_kv3[:, :], start=True, stop=True)
                            mm.then_inc(RT["kv_ps"], 1)
                        if f is not None:
                            wait(pe, FF["hid_sb"], f * 3 + 2)
                            wait(pe, BN["gates"], f - 1)
                            pe.matmul(bank["J1"][:, 0:256], w_exp[:, 1, 0:HID], hidT[:, 1, :], start=True, stop=True).then_inc(FF["hid_ps"], 1)
                    if k == 4:
                        if r is not None:
                            wait(pe, RT["qk_sb"], r + 1)
                            for t in range(2):
                                mm = pe.matmul(bank["OT"][:, t * P:(t + 1) * P], qk3[:, 256 + t * P:256 + (t + 1) * P], qk3[:, t * P:(t + 1) * P],
                                               start=True, stop=True)
                            mm.then_inc(RT["s_ps"], 1)
                        if f is not None:
                            wait(pe, FF["hid_sb"], f * 3 + 3)
                            for t in range(2):
                                pe.matmul(bank["J1"][:, t * C:(t + 1) * C], hidT[:, 2, t * P:(t + 1) * P], w_o[:, :], start=True, stop=False)
                                mm = pe.matmul(bank["J1"][:, t * C:(t + 1) * C], ones_row[:, :], b_o[:, :], start=False, stop=True)
                            mm.then_inc(FF["out_ps"], 1)
                    if k == 6 and r is not None:
                        wait(pe, RT["kd"], r + 1)
                        wait(pe, RT["v"], r + 1)
                        wait(pe, RT["sd"], r + 1)
                        wait(pe, RT["qd"], r + 1)
                        wait(pe, RT["reset"], r + 1)
                        for t in range(2):
                            if t:
                                wait(pe, RT["state"], r * 2 + 1)
                                settle(pe)
                            pe.matmul(bank["T"][0:C, 0:C], kd3[:, t, :], v3[:, t, :], start=True, stop=True).then_inc(RT["kv_sum"], 1)
                            pe.matmul(bank["OT"][:, t * C:(t + 1) * C], sd3[:, t, :], v3[:, t, :], start=True, stop=False)
                            mm = pe.matmul(bank["OT"][:, t * C:(t + 1) * C], qd3[:, t * P:(t + 1) * P], state[:, t, :], start=False, stop=True)
                        mm.then_inc(RT["out_ps"], 1)
                if q is not None:
                    reduce(7)

            staggered(pe, strips)

        @block.scalar
        def _(act):
            def neg_max(c, i):
                q = c["s"]
                wait(act, q["maxT"], i + 1)
                act.activation(mT[:, :], bank["T"][:, 0:P], ACT.Copy, scale=-1.0).then_inc(q["negmax"], 1)

            def attention(c, i):
                q, nk, ng = c["s"], c["nk"], c["ng"]
                neg_max(c, i)
                for g in range(ng):
                    wait(act, q["scores"], i * ng + g + 1)
                    wait(act, q["av_done"], i * ng + g + 1)
                    act.activation(prob[0:nk, g % 2, :], S[g % 2][0:nk, :], ACT.Exp).then_inc(q["exp_done"], 1)
                wait(act, q["sel_done"], (i + 1) * ng + 2)
                n = c["np"] * NQ
                act.activation(aT[0:C, 0:n], bank["OT"][0:C, 0:n], ACT.Copy).then_inc(q["attn_out"], 1)

            act.wait_ge(s_w, 16 * NLOADS)
            act.wait_ge(s_const, NCONST)
            act.activation(rstd_warm[:, :], ident[:, 0:1], ACT.Exp)
            act.sem_inc(T1["exp_done"], 2)
            act.sem_inc(T2["exp_done"], 2)
            act.sem_inc(BN["sign"], 2)
            act.sem_inc(L["xT_sb"], 1)
            with act.Fori(0, NT) as i:
                wait(act, T1["xT_ps"], i + 1)
                act.activation(xT[0:C, :].rearrange("c (n r w) -> c n r w", n=8, r=WIN),
                               bank["T"][0:C, :].rearrange("c (r n w) -> c n r w", n=8, r=WIN), ACT.Copy).then_inc(T1["xT_sb"], 1)
                wait(act, T1["v_ps"], i + 1)
                act.activation(vsb[0:NKT, 0:8, 0:C], bank["OT"][0:NKT, :].rearrange("p (n c) -> p n c", c=C), ACT.Copy).then_inc(T1["v_sb"], 1)
                attention(TOKC, i)
            with act.Fori(0, NT) as i:
                wait(act, L["xT_ps"], i + 1)
                wait(act, L["stored"], i * 48)
                act.activation(xpad[0:C, :].rearrange("c (r w) -> c r w", w=PW)[:, :, HALF:HALF + W],
                               bank["T"][0:C, :].rearrange("c (r w) -> c r w", w=W), ACT.Copy).then_inc(L["xT_sb"], 1)
                wait(act, L["k_ps"], i + 1)
                act.activation(kpad[:, :].rearrange("c (r w) -> c r w", w=PW)[:, :, HALF:HALF + W],
                               bank["J1"][0:C, :].rearrange("c (r w) -> c r w", w=W), ACT.Copy).then_inc(L["k_sb"], 1)
            with act.Fori(0, NS) as i:
                for hf in range(2):
                    wait(act, T2["v_ps"], i * 2 + hf + 1)
                    act.activation(vsb[0:NKL, hf * 8:hf * 8 + 8, 0:C], bank["OT"][0:NKL, :].rearrange("p (n c) -> p n c", c=C), ACT.Copy).then_inc(T2["v_sb"], 1)
                attention(LOCC, i)

            def strips(j, par):
                f, r, g, q = (inside(j - k) for k in range(4))
                for k in range(8):
                    if q is not None:
                        wait(act, BN["w_ps"], q * 8 + k + 1)
                        wait(act, BN["prod"], q * 8 + k - 1)
                        act.activation(sgn[:, k % 2, :], double[k % 2][:, :], ACT.Sign).then_inc(BN["sign"], 1)
                    if k == 1:
                        if f is not None:
                            wait(act, FF["xT_ps"], f + 1)
                            act.activation(xnT[0][0:C, :], bank["T"][0:C, 0:256], ACT.Copy).then_inc(FF["xT_sb"], 1)
                    if k == 2:
                        if f is not None:
                            wait(act, FF["hid_ps"], f * 3 + 1)
                            wait(act, FF["out_ps"], f)
                            act.activation(hidT[:, 0, :], bank["J1"][:, 0:256], ACT.Relu).then_inc(FF["hid_sb"], 1)
                        if r is not None:
                            wait(act, RT["xT_ps"], r + 1)
                            act.activation(xnT[1][0:C, :], bank["T"][0:C, 0:256], ACT.Copy).then_inc(RT["xT_sb"], 1)
                    if k == 3:
                        if f is not None:
                            wait(act, FF["hid_ps"], f * 3 + 2)
                            act.activation(hidT[:, 1, :], bank["J1"][:, 0:256], ACT.Relu, bias=w_exp[:, 0, HID:HID + 1]).then_inc(FF["hid_sb"], 1)
                        if g is not None:
                            wait(act, BN["xT_ps"], g + 1)
                            wait(act, BN["prod"], (g - 1) * 8)
                            act.activation(xnT[2][0:C, :], bank["T"][0:C, 0:256], ACT.Copy).then_inc(BN["xT_sb"], 1)
                            act.activation(xb2[:, par, :], bank["T"][:, 0:256], ACT.Sign).then_inc(BN["xb"], 1)
                        if r is not None:
                            wait(act, RT["qk_ps"], r + 1)
                            act.activation(qk3[0:C, :], bank["OT"][0:C, :], ACT.Copy).then_inc(RT["qk_sb"], 1)
                    if k == 4:
                        if f is not None:
                            wait(act, FF["hid_ps"], f * 3 + 3)
                            act.activation(hidT[:, 2, :], bank["J1"][:, 0:256], ACT.Relu, bias=w_exp[:, 1, HID:HID + 1]).then_inc(FF["hid_sb"], 1)
                        if r is not None:
                            wait(act, RT["kv_ps"], r + 1)
                            wait(act, RT["kd"], r + 1)
                            act.activation(v3[:, :, :], bank["T"][:, 0:256].rearrange("p (t n) -> p t n", t=2)[:, :, C:2 * C], ACT.Copy).then_inc(RT["v"], 1)

            staggered(act, strips)

        @block.vector
        def _(dve):
            def attention(c, i):
                q, nk, ng = c["s"], c["nk"], c["ng"]
                wait(dve, q["maxT"], i)
                for g in range(ng):
                    wait(dve, q["max_scores"], i * ng + g + 1)
                    dve.tensor_reduce(m_sb[:, g * GP:(g + 1) * GP], bank["MX"][:, 0:GP * nk].rearrange("p (u n) -> p u n", u=GP),
                                      AX.X, ALU.max).then_inc(q["max_done"], 1)
                for g in range(ng):
                    v = bank["AV"][:, :].rearrange("p (u n) -> p u n", u=GP)
                    wait(dve, q["av_done"], i * ng + g + 3)
                    wait(dve, q["sel_done"], i * ng + g + 1)
                    dve.reciprocal(rec[:, g % 2, :], v[:, :, C]).then_inc(q["rec_done"], 1)
                    dve.tensor_tensor(msk[:, g % 2, :].rearrange("p (u n) -> p u n", u=GP), v[:, :, 0:C],
                                      headmask[:, :].rearrange("p (a n) -> p a n", a=1).broadcast_to((P, GP, C)), ALU.mult).then_inc(q["norm_done"], 1)
                    wait(dve, q["rec_done"], i * ng + g + 1)
                    dve.tensor_tensor(selr[:, g % 2, :].rearrange("p (u n) -> p u n", u=GP),
                                      sel[:, :].rearrange("p (a n) -> p a n", a=1).broadcast_to((P, GP, NQ)),
                                      rec[:, g % 2, :].rearrange("p (u a) -> p u a", a=1).broadcast_to((P, GP, NQ)), ALU.mult).then_inc(q["norm_done"], 1)

            def moments(name, q, i, src):
                stats, mv, veps, _ = ln_sb[name]
                n = stats.shape[1]
                for t in range(n):
                    dve.bn_stats(stats[:, t, :], src(t)).then_inc(q["stats"], 1)
                for t in range(n):
                    wait(dve, q["stats"], i * n + t + 1)
                    settle(dve)
                    dve.bn_aggr(mv[:, t, :], stats[:, t, :]).then_inc(q["mv"], 1)
                wait(dve, q["mv"], (i + 1) * n)
                dve.tensor_scalar(veps[:, :], mv[:, :, 1], EPS, None, ALU.add).then_inc(q["veps"], 1)

            def normalize(name, q, i, src, dst):
                _, mv, _, rstd = ln_sb[name]
                wait(dve, q["rstd"], i + 1)
                wait(dve, q["xT_ps"], i)
                for t in range(mv.shape[1]):
                    s = src(t)
                    d = dst(t)
                    if len(d.shape) == 3:
                        s = s.rearrange("p (a c) -> p a c", a=1).broadcast_to((P, 2, C))
                    dve.tensor_scalar(d, s, mv[:, t, 0:1], rstd[:, t:t + 1], ALU.subtract, ALU.mult).then_inc(q["xn"], 1)

            def rows(t0, n):
                return h[:, bass.ds(t0, n), :]

            def row(t0):
                return lambda t: h[:, bass.ds(t0 + t, 1), :].rearrange("p a c -> p (a c)")

            dve.sem_inc(T1["av_done"], 2)
            dve.sem_inc(T2["av_done"], 2)
            dve.sem_inc(T1["sel_done"], 2)
            dve.sem_inc(T2["sel_done"], 2)
            dve.wait_ge(s_w, 16 * NLOADS)
            dve.wait_ge(s_const, NCONST)
            dve.tensor_copy(route_f[:, :], route_i[:, :]).then_inc(s_parts, 1)
            dve.tensor_copy(onehot[0:32, :], onehot_f[:, :]).then_inc(s_prep, 1)
            dve.tensor_tensor(shared[:, :, 0:HID], shared[:, :, 0:HID],
                              ident[:, :].rearrange("p (a n) -> p a n", a=1).broadcast_to((P, NLAY, P)), ALU.add).then_inc(s_route, 1)
            dve.wait_ge(s_route, 1)
            for l in range(NLAY):
                dve.tensor_tensor(experts[:, l, :, :], experts[:, l, :, :],
                                  shared[:, l, :].rearrange("p (a n) -> p a n", a=1).broadcast_to((P, NEXP + 1, HID + 1)), ALU.add).then_inc(s_prep, 1)
            dve.tensor_scalar(route_ok[:, :], route_i[:, :], 0.0, None, ALU.is_ge).then_inc(s_route, 1)
            dve.wait_ge(s_route, 2)
            dve.scalar_tensor_tensor(out=route_ok[:, :], in0=route_i[:, :], scalar=float(NEXP), in1=route_ok[:, :], op0=ALU.is_lt, op1=ALU.mult).then_inc(s_route, 1)
            dve.wait_ge(s_route, 3)
            dve.scalar_tensor_tensor(out=route_f[:, :], in0=route_i[:, :], scalar=-float(NEXP), in1=route_ok[:, :], op0=ALU.add, op1=ALU.mult).then_inc(s_parts, 1)
            dve.wait_ge(s_parts, 2)
            dve.tensor_scalar(route_x[:, :], route_f[:, :], float(NEXP), None, ALU.add).then_inc(s_route, 1)
            dve.tensor_copy(w_3[:, 0, :], w_bin[:, :]).then_inc(s_parts, 1)
            dve.wait_ge(s_parts, 3)
            dve.tensor_tensor(w_rest[:, :], w_bin[:, :], w_3[:, 0, :], ALU.subtract).then_inc(s_moved, 1)
            dve.wait_ge(s_moved, 1)
            dve.tensor_copy(w_3[:, 1, :], w_rest[:, :]).then_inc(s_parts, 1)
            dve.wait_ge(s_parts, 4)
            dve.tensor_tensor(w_3[:, 2, :], w_rest[:, :], w_3[:, 1, :], ALU.subtract).then_inc(s_parts, 1)
            dve.tensor_copy(pair_sel[:, :], pair_f[:, :]).then_inc(s_moved, 1)

            with dve.Fori(0, NT) as i:
                wait(dve, T1["qk_ps"], i + 1)
                wait(dve, T1["q_in"], i * 16 * NH)
                dve.tensor_tensor(t_cos[:, :], bank["J1"][:, :], cos[:, :], ALU.mult).then_inc(T1["rope_mul"], 1)
                dve.tensor_tensor(t_sin[:, :], bank["J2"][:, :], sin[:, :], ALU.mult).then_inc(T1["rope_mul"], 1)
                wait(dve, T1["rope_mul"], (i + 1) * 2)
                wait(dve, T1["scores"], i * TOKC["ng"])
                dve.tensor_tensor(rot[0:C, :], t_cos[0:C, :], t_sin[0:C, :], ALU.add).then_inc(T1["rope"], 1)
                for pc in range(2):
                    def half(b):
                        return b[C:2 * C, :].rearrange("k (n r p c) -> k p n r c", n=16, r=QP, p=2)[:, pc, :, :, :]
                    dve.tensor_tensor(rot[C:2 * C, :].rearrange("k (n p r c) -> k p n r c", n=16, r=QP, p=2)[:, pc, :, :, :],
                                      half(t_cos), half(t_sin), ALU.add).then_inc(T1["rope"], 1)
                attention(TOKC, i)
                wait(dve, T1["proj"], i + 1)
                dve.tensor_copy(rows(i * 4, 4), bank["J2"][:, 0:256].rearrange("p (t c) -> p t c", t=4)).then_inc(T1["h_done"], 1)
            wait(dve, T1["h_done"], NT)
            with dve.Fori(0, NT) as i:
                moments("pre", L, i, row(i * 4))
                normalize("pre", L, i, row(i * 4), lambda t: xn[:, t, :])
                wait(dve, L["q_ps"], i + 1)
                wait(dve, L["stored"], i * 48)
                for t in range(2):
                    dve.tensor_scalar(q_sb[:, t * 256:(t + 1) * 256].rearrange("c (p r w) -> c p r w", p=16, r=QP),
                                      bank["J2"][0:C, t * 256:(t + 1) * 256].rearrange("c (r p w) -> c p r w", p=16, r=QP),
                                      temp[:, :], float(HD ** -0.5), ALU.mult, ALU.mult).then_inc(L["q_sb"], 1)
            with dve.Fori(0, NS) as i:
                attention(LOCC, i)
                wait(dve, T2["proj"], i + 1)
                dve.tensor_tensor(rows(i * 2, 2), bank["J2"][:, 0:128].rearrange("p (t c) -> p t c", t=2), rows(i * 2, 2), ALU.add).then_inc(T2["h_done"], 1)
            wait(dve, T2["h_done"], NS)

            def add_rows(i, ps, q):
                dve.tensor_tensor(rows(i * 2, 2), bank[ps][:, 0:128].rearrange("p (t c) -> p t c", t=2), rows(i * 2, 2), ALU.add).then_inc(q["h_done"], 1)

            def strips(j, par):
                f, r, g, q = (inside(j - k) for k in range(4))
                if f is not None:
                    moments("ffn", FF, f, row(f * 2))
                for k in range(8):
                    if q is not None:
                        wait(dve, BN["sign"], q * 8 + k + 3)
                        wait(dve, BN["y_part"], q * 8 + k - 1)
                        dve.tensor_tensor(prod[:, k % 2, :].rearrange("p (u n) -> p u n", u=4), sgn[:, k % 2, :].rearrange("p (u n) -> p u n", u=4),
                                          xb2[:, 1 - par:2 - par, :].broadcast_to((P, 4, 256)), ALU.mult).then_inc(BN["prod"], 1)
                    if k == 0:
                        if f is not None:
                            normalize("ffn", FF, f, row(f * 2), lambda t: xn_f[:, t, :])
                        if r is not None:
                            wait(dve, FF["h_done"], r + 1)
                            settle(dve)
                            moments("ret", RT, r, row(r * 2))
                    if k == 1:
                        if r is not None:
                            normalize("ret", RT, r, row(r * 2), lambda t: xn_r[:, t, :])
                            wait(dve, RT["state"], r * 2)
                            dve.tensor_scalar(state[0:C, 0, :], state[0:C, 0, :], keep[0:C, bass.ds(r, 1)], None, ALU.mult).then_inc(RT["reset"], 1)
                        if g is not None:
                            wait(dve, RT["h_done"], g + 1)
                            settle(dve)
                            moments("bin", BN, g, row(g * 2))
                    if k == 2 and g is not None:
                        normalize("bin", BN, g, row(g * 2), lambda t: xn2[:, t, :, :])
                    if k == 3:
                        if g is not None:
                            wait(dve, BN["g_ps"], g + 1)
                            wait(dve, BN["w_ps"], (g - 1) * 8)
                            dve.tensor_scalar(g3[0:3 * NG, par, :], bank["J1"][0:3 * NG, 0:256], 0.0, None, ALU.is_gt).then_inc(BN["gates"], 1)
                    if k == 4:
                        if r is not None:
                            wait(dve, RT["kv_ps"], r + 1)
                            wait(dve, RT["out_ps"], r)
                            dve.tensor_scalar(kd3[:, :, :], bank["T"][:, 0:256].rearrange("p (t n) -> p t n", t=2)[:, :, 0:C],
                                              decay_k[:, :], None, ALU.mult).then_inc(RT["kd"], 1)
                            wait(dve, RT["qk_sb"], r + 1)
                            dve.tensor_tensor(qd3[0:C, :], qk3[0:C, 0:256], decay_q[:, :], ALU.mult).then_inc(RT["qd"], 1)
                    if k == 5:
                        if r is not None:
                            wait(dve, RT["s_ps"], r + 1)
                            dve.tensor_tensor(sd3[:, :, :], bank["OT"][:, 0:256].rearrange("p (t n) -> p t n", t=2),
                                              decay[:, :].rearrange("p (a n) -> p a n", a=1).broadcast_to((P, 2, P)), ALU.mult).then_inc(RT["sd"], 1)
                        if f is not None:
                            wait(dve, FF["out_ps"], f + 1)
                            add_rows(f, "J1", FF)
                    if k == 6 and r is not None:
                        for t in range(2):
                            wait(dve, RT["kv_sum"], r * 2 + t + 1)
                            wait(dve, RT["reset"], r + 1)
                            if t == 1:
                                wait(dve, RT["state"], r * 2 + 1)
                                wait(dve, RT["out_ps"], r + 1)
                            dve.scalar_tensor_tensor(out=state[0:C, 1 - t, :], in0=state[0:C, t, :], scalar=float(ALPHA ** P),
                                                     in1=bank["T"][0:C, 0:C], op0=ALU.mult, op1=ALU.add).then_inc(RT["state"], 1)
                        add_rows(r, "OT", RT)
                if q is not None:
                    wait(dve, BN["y_part"], (q + 1) * 8)
                    wait(dve, BN["y"], q)
                    dve.tensor_tensor(ys[:, :, :], bank["AV"][:, 0:128].rearrange("p (t c) -> p t c", t=2),
                                      scale_bc[:, :].rearrange("p (a n) -> p a n", a=1).broadcast_to((P, 2, C)), ALU.mult).then_inc(BN["y_scaled"], 1)
                    wait(dve, BN["y_scaled"], q + 1)
                    wait(dve, BN["stored"], q * 16)
                    dve.tensor_tensor(yo[:, :, :], ys[:, :, :], rows(q * 2, 2), ALU.add).then_inc(BN["y"], 1)

            staggered(dve, strips)


NLOADS = 32
NSTRIP = TOK // 256
NCONST = 30


def _with_bias(w, b):
    return np.concatenate([w, b[None, :]], 0)


def kernel(x, L0_tok_qkv_w, L0_tok_qkv_b, L0_tok_proj_w, L0_tok_proj_b, L0_attn_W_qkv, L0_attn_W_proj, L0_attn_b_proj,
           L0_attn_temperature, L0_ffn_route_id, L0_ffn_Wi, L0_ffn_bi, L0_ffn_Wr, L0_ffn_br, L0_ffn_Ws, L0_ffn_bs, L0_ffn_Wo,
           L0_ffn_bo, L1_attn_Wqkv, L1_attn_bqkv, L1_ffn_weight, L1_ffn_proj_w, L1_ffn_proj_b, L1_ffn_scale):
    import concourse.bacc as _bacc
    from concourse.bass_utils import run_bass_kernel_spmd as _run

    n = np.asarray
    arr = {k: v for k, v in shape_tables().items()}
    arr["pair"] = (np.arange(P)[:, None] // C == np.arange(2)[None, :]).astype(np.float32)
    arr["x"] = n(x)
    w, b = n(L0_tok_qkv_w), n(L0_tok_qkv_b)
    order = np.concatenate([np.arange(C) + C, np.arange(C)])
    arr["w_qk"] = _with_bias(w[order].T, b[order])
    arr["w_qk_swap"] = _with_bias(w[order ^ 1].T, b[order ^ 1])
    arr["w_v1"] = _with_bias(w[2 * C:].T, b[2 * C:])
    arr["w_p1"] = _with_bias(n(L0_tok_proj_w).T, n(L0_tok_proj_b))
    w = n(L0_attn_W_qkv)
    arr["w_q2"], arr["w_k2"], arr["w_v2"] = w[:C].T, w[C:2 * C].T, w[2 * C:].T
    arr["w_p2"] = _with_bias(n(L0_attn_W_proj).T, n(L0_attn_b_proj))
    arr["temp"] = n(L0_attn_temperature).reshape(1, 1)
    arr["w_i"] = _with_bias(n(L0_ffn_Wi).T, n(L0_ffn_bi))
    wr, br, ws, bs = n(L0_ffn_Wr), n(L0_ffn_br), n(L0_ffn_Ws), n(L0_ffn_bs)
    arr["experts"] = np.concatenate([wr.transpose(3, 0, 1, 2), br.transpose(2, 0, 1)[..., None]], 3)
    arr["shared"] = np.concatenate([ws[:, 0].transpose(2, 0, 1), bs[:, 0].T[..., None]], 2)
    arr["w_o"], arr["b_o"] = n(L0_ffn_Wo).T, n(L0_ffn_bo).reshape(1, C)
    arr["route"] = n(L0_ffn_route_id).reshape(1, -1)
    w, b = n(L1_attn_Wqkv), n(L1_attn_bqkv)
    arr["w_q3"], arr["w_k3"] = _with_bias(w[:, :C], b[:C]), _with_bias(w[:, C:2 * C], b[C:2 * C])
    arr["w_kv3"] = _with_bias(w[:, C:], b[C:])
    g = _with_bias(n(L1_ffn_proj_w).T, n(L1_ffn_proj_b))
    arr["w_gate"] = np.concatenate([g, g, g], 1)
    arr["w_bin"] = n(L1_ffn_weight)[0].reshape(NG, C, C // 2, 2).transpose(0, 2, 3, 1).reshape(P, -1)
    arr["scale"] = n(L1_ffn_scale).reshape(1, C)

    nc = _bacc.Bacc("TRN2", target_bir_lowering=False, num_devices=1)
    arrays, aps = {}, {}
    for k in ("w_qk", "w_qk_swap", "w_v1", "w_p1", "w_q2", "w_k2", "w_v2", "w_p2", "w_i", "b_o", "w_q3", "w_k3", "w_kv3", "w_gate"):
        arr[k] = np.pad(arr[k], ((0, P - arr[k].shape[0]), (0, 0)))
    for k, v in arr.items():
        v = np.ascontiguousarray(v)
        arrays["in_" + k] = v
        aps[k] = nc.dram_tensor("in_" + k, v.shape, mybir.dt.from_np(v.dtype), kind="ExternalInput").ap()
    o = nc.dram_tensor("out_0", (B, H * W, C), F32, kind="ExternalOutput").ap()
    build(nc, aps, o)
    return _run(nc, [arrays], core_ids=[0]).results[0]["out_0"]
```

```python
from contextlib import ExitStack

import numpy as np
import concourse.bass as bass
from concourse import mybir

F32 = mybir.dt.float32
BF16 = mybir.dt.bfloat16
I32 = mybir.dt.int32
ALU = mybir.AluOpType
ACT = mybir.ActivationFunctionType
AX = mybir.AxisListType

P = 128
B, H, W, C = 4, 64, 64, 64
NH, HD = 8, 8
TOK = B * H * W
TILES = TOK // P
WIN = 8
QP = 4
NQ = QP * QP
HALF = 3
KS = QP + 2 * HALF
NKL = KS * KS
NKT = WIN * WIN
PW = W + 2 * HALF
CMOD = 12
NAUG = KS + CMOD + 1
BIG = 1.0e9
HID, NEXP, NLAY = 128, 16, 2
KL_ROWS = C + NAUG
NG = 8
EPS = 1e-5
ALPHA = 0.99
STRIPS = H // QP
GP = 4


def shape_tables():
    t = {}
    t["ident"] = np.eye(P, dtype=np.float32)
    ch = np.arange(C)
    d = ch % HD
    half = HD // 2
    freq = (1.0 / 10000.0 ** (np.arange(0, half, 2, dtype=np.float32) / half)).astype(np.float32)
    f = freq[(d % half) // 2]
    wpos = np.arange(WIN * W)
    pos = np.where((d < half)[:, None], (wpos // WIN % WIN)[None, :], (wpos % WIN)[None, :])
    ang = (pos.astype(np.float32) * f[:, None]).astype(np.float32)
    cos, sin = np.cos(ang), np.sin(ang) * np.where(d % 2 == 0, -1.0, 1.0)[:, None]
    scale = np.float32(HD ** -0.5)
    t["cos"] = np.concatenate([cos, cos * scale]).astype(np.float32)
    t["sin"] = np.concatenate([sin, sin * scale]).astype(np.float32)
    hq = np.arange(P)
    t["headmask"] = (hq[:, None] // NQ == ch[None, :] // HD).astype(np.float32)
    t["sel"] = (hq[:, None] % NQ == np.arange(NQ)[None, :]).astype(np.float32)
    t["onehot"] = np.repeat(np.eye(32, dtype=np.float32)[:, :, None], NKL, 2).reshape(32, -1)
    aug = np.zeros((STRIPS, NAUG, KS, PW), np.float32)
    for r in range(KS):
        aug[:, r, r, :] = 1
    for c in range(PW):
        aug[:, KS + c % CMOD, :, c] = 1
        if c < HALF or c >= PW - HALF:
            aug[:, KS + CMOD, :, c] = 1
    aug[0, KS + CMOD, :HALF, :] = 1
    aug[STRIPS - 1, KS + CMOD, KS - HALF:, :] = 1
    t["kaug"] = aug.reshape(STRIPS, NAUG, KS * PW)
    qa = np.zeros((NAUG, QP, W), np.float32)
    for r in range(QP):
        for kr in range(KS):
            if abs(kr - HALF - r) > HALF:
                qa[kr, r, :] = -BIG
    for c in range(W):
        j = c // QP
        for kc in range(KS):
            if abs(kc - HALF - c % QP) > HALF:
                qa[KS + (QP * j + kc) % CMOD, :, c] = -BIG
    qa[KS + CMOD] = -BIG
    qa = qa.reshape(NAUG, QP, W // QP, QP).transpose(0, 2, 1, 3).reshape(NAUG, W // QP, 1, NQ)
    t["qaug"] = np.repeat(qa, NH, 2).reshape(NAUG, -1)
    i = np.arange(P, dtype=np.float64)
    dm = np.where(i[None, :] >= i[:, None], ALPHA ** (i[None, :] - i[:, None]), 0.0) / np.sqrt(C)
    t["decay"] = dm.astype(np.float32)
    t["decay_q"] = np.tile((ALPHA ** (i + 1) / np.sqrt(C))[None, :], (C, 2)).astype(np.float32)
    t["keep"] = np.repeat((np.arange(TOK // 256) % STRIPS != 0).astype(np.float32)[None, :], P, 0)
    t["decay_k"] = (ALPHA ** (P - 1 - i))[:, None].astype(np.float32)
    return t


def build(nc, a, out):
    ctx = ExitStack()
    with ctx:
        def sb(name, shape, dt=F32):
            return ctx.enter_context(nc.sbuf_tensor(name, shape, dt))

        def sem(name):
            return ctx.enter_context(nc.semaphore(name))

        bank = {n: ctx.enter_context(nc.psum_tensor("ps_" + n, [P, 512], F32)) for n in ("T", "J1", "AV", "OT")}
        double = [ctx.enter_context(nc.psum_tensor("ps_D%d" % n, [P, 1024], F32)) for n in range(2)]
        bank["J2"], bank["MX"] = double[0][:, 0:512], double[0][:, 512:1024]
        bank["S0"], bank["S1"] = double[1][:, 0:512], double[1][:, 512:1024]

        h = sb("h", [P, TILES, C])
        ident = sb("ident", [P, P])
        cos, sin = sb("cos", [P, 512]), sb("sin", [P, 512])
        headmask, sel = sb("headmask", [P, C]), sb("sel", [P, NQ])
        onehot_f = h[0:32, 0:32 * NKL // C, :].rearrange("p t c -> p (t c)")
        onehot = sb("onehot", [P, 32 * NKL], BF16)
        decay, decay_q, decay_k = sb("decay", [P, P]), sb("decay_q", [C, 256]), sb("decay_k", [P, 1])
        w_qk, w_qk_swap, w_v1, w_p1 = sb("w_qk", [P, 128]), sb("w_qk_swap", [P, 128]), sb("w_v1", [P, C]), sb("w_p1", [P, C])
        w_q2, w_k2, w_v2, w_p2 = sb("w_q2", [P, C]), sb("w_k2", [P, C]), sb("w_v2", [P, C]), sb("w_p2", [P, C])
        temp = sb("temp", [C, 1])
        w_i = sb("w_i", [P, HID])
        experts = sb("experts", [P, NLAY, NEXP + 1, HID + 1])
        shared = sb("shared", [P, NLAY, HID + 1])
        w_o, b_o, ones_row = sb("w_o", [P, C]), sb("b_o", [P, C]), sb("ones_row", [P, P])
        w_q3, w_k3, w_kv3 = sb("w_q3", [P, C]), sb("w_k3", [P, C]), sb("w_kv3", [P, 128])
        w_gate = sb("w_gate", [P, 3 * NG])
        w_bin, w_rest = sb("w_bin", [P, C * C * NG // P]), sb("w_rest", [P, C * C * NG // P])
        w_3 = sb("w_3", [P, 3, C * C * NG // P], BF16)
        w_parts = sb("w_parts", [P, C * C], BF16)
        pair_sel = sb("pair_sel", [P, 2], BF16)
        pair_f = sb("pair_f", [P, 2])
        scale_bc = sb("scale_bc", [P, C])
        route_i, route_f, route_ok, route_x = sb("route_i", [1, 64], I32), sb("route_f", [1, 64]), sb("route_ok", [1, 64]), sb("route_x", [1, 64], I32)
        minus_half = sb("minus_half", [P, 4])
        zeros = sb("zeros", [C, HALF * PW])

        xin = sb("xin", [P, 4, C])
        xT = sb("xT", [P, 512])
        t_cos, t_sin, rot = sb("t_cos", [P, 512]), sb("t_sin", [P, 512]), sb("rot", [P, 512])
        qexp = sb("qexp", [P, NH * 512])
        q_blocks = qexp[:, :].rearrange("k (p h q) -> k p h q", h=NH, q=NQ)
        kpatch, xpatch = sb("kpatch", [P, 2, 16 * NKL]), sb("xpatch", [P, 2, 16 * NKL])
        kst, xst = sb("kst", [P, KS * PW]), sb("xst", [C, KS * PW])
        vsb = sb("vsb", [P, 2, 16, P])
        m_sb, mT = sb("m_sb", [P, P]), sb("mT", [P, 2, P], BF16)
        prob = sb("prob", [P, 2, 512])
        rec, selr, msk = sb("rec", [P, 2, GP]), sb("selr", [P, 2, GP * NQ]), sb("msk", [P, 2, GP * C])
        aT = sb("aT", [P, 512])
        rstd_warm = sb("table_warm", [P, 1])
        xn = sb("xn", [P, 4, C])
        xpad, kpad, q_sb = sb("xpad", [P, WIN * PW]), sb("kpad", [C, WIN * PW]), sb("q_sb", [C, 512])
        xnT = [sb("xnT%d" % n, [P, 256]) for n in range(3)]
        ln_sb = {}
        for n, t in (("pre", 4), ("ffn", 2), ("ret", 2), ("bin", 2)):
            ln_sb[n] = (sb("stats_" + n, [P, t, 6]), sb("mv_" + n, [P, t, 2]), sb("veps_" + n, [P, t]), sb("rstd_" + n, [P, t]))
        xn_f, xn_r = sb("xn_f", [P, 2, C]), sb("xn_r", [P, 2, C])
        keep = sb("keep", [P, NSTRIP])
        hidT = sb("hidT", [P, 3, 256])
        w_exp = sb("w_exp", [P, NLAY, HID + 1])
        qk3, qd3 = sb("qk3", [P, 512]), sb("qd3", [P, 256])
        kd3, v3, sd3 = sb("kd3", [P, 2, C]), sb("v3", [P, 2, C]), sb("sd3", [P, 2, P])
        state = sb("state", [P, 2, C])
        xn2 = sb("xn2", [P, 2, 2, C])
        xb2 = sb("xb2", [P, 2, 256], BF16)
        g3 = sb("g3", [P, 2, 256], BF16)
        sgn, prod = sb("sgn", [P, 2, 1024], BF16), sb("prod", [P, 2, 1024], BF16)
        ys, yo = sb("ys", [P, 2, C]), sb("yo", [P, 2, C])

        kx_d = nc.dram_tensor("kx_d", (B, 2, C, PW * PW), F32, kind="Internal").ap()
        qs_d = nc.dram_tensor("qs_d", (C, TOK), F32, kind="Internal").ap()
        x_v = a["x"].rearrange("b (t y) w c -> (y w) (b t) c", y=2)
        o_v = out.rearrange("b (t p) c -> p (b t) c", p=P)

        s_w = sem("weights_loaded")
        s_const = sem("constants_made")
        s_prep = sem("experts_combined")
        s_route = sem("routes_ready")
        s_parts = sem("gate_weights_split")
        s_moved = sem("gate_weight_parts_moved")

        def named(prefix, *names):
            return {n: sem(prefix + "_" + n) for n in names}

        def times(count, most=None):
            if isinstance(count, int):
                return max(min(count, most) if most else count, 0) + 1
            return count + 1

        s_settled = sem("settled")

        def settle(eng):
            eng.sem_inc(s_settled, 1)

        core = ("max_scores", "max_done", "maxT", "negmax", "scores", "exp_done", "av_done", "rec_done",
                "norm_done", "sel_done", "attn_out", "v_ps", "v_sb", "q_in", "k_in", "x_patch", "k_patch", "proj", "h_done")
        T1 = named("tok", "x_in", "xT_ps", "xT_sb", "qk_ps", "rope_mul", "rope", *core)
        T2 = named("loc", *core)
        L = named("pre", "stats", "mv", "veps", "rstd", "xn", "xT_ps", "xT_sb", "k_ps", "q_ps", "k_sb", "q_sb", "stored", "padded")
        FF = named("ffn", "stats", "mv", "veps", "rstd", "xn", "xT_ps", "xT_sb", "w_in", "hid_ps", "hid_sb", "out_ps", "h_done")
        RT = named("ret", "stats", "mv", "veps", "rstd", "xn", "xT_ps", "xT_sb", "qk_ps", "qk_sb", "kv_ps", "kd", "v", "qd", "s_ps",
                   "sd", "kv_sum", "state", "reset", "out_ps", "h_done")
        BN = named("bin", "stats", "mv", "veps", "rstd", "xn", "xT_ps", "xb", "xT_sb", "g_ps", "gates", "w_ps", "sign", "prod",
                   "y_part", "y_ps", "y_scaled", "y", "stored")

        def operand(buf, n, at, narrow):
            if narrow:
                return buf[:, at * n:(at + 1) * n].bitcast(BF16).rearrange("p (n e) -> p n e", e=2)[:, :, 1]
            return buf[:, at * n:(at + 1) * n]

        KL = C + NAUG
        q_half = [qexp[:, par * NH * 256:(par + 1) * NH * 256] for par in range(2)]

        def tok_at(p):
            return QP * (p // 2 % 2), WIN * (p // 4) + QP * (p % 2)

        def loc_at(p):
            return 0, QP * p

        TOKC = dict(nv=1, s=T1, nk=NKT, np=32, ng=8, credit=0, kv=P, at=tok_at,
                    q=lambda par, p, narrow: operand(qexp, P, p, narrow),
                    k=lambda par, p, narrow: operand(rot, NKT, p // 4, narrow), v=lambda par, p: vsb[:, par, p // 4, :])
        LOCC = dict(nv=2, s=T2, nk=NKL, np=16, ng=4, credit=4, kv=NKL, at=loc_at,
                    q=lambda par, p, narrow: operand(q_half[par], P, p, narrow),
                    k=lambda par, p, narrow: operand(kpatch[:, par, :], NKL, p, narrow), v=lambda par, p: vsb[0:NKL, par, p, :])
        onehot_v = onehot[:, :].rearrange("k (p n) -> k p n", p=32)
        S = [bank["S0"], bank["S1"]]

        def inside(i):
            return i if not isinstance(i, int) or 0 <= i < NSTRIP else None

        def staggered(eng, strips):
            for j in range(3):
                strips(j, j % 2)
            with eng.Fori(3, NSTRIP - 1, 2) as j:
                strips(j, 1)
                strips(j + 1, 0)
            for j in range(NSTRIP - 1, NSTRIP + 3):
                strips(j, j % 2)

        def strips_ahead(eng, front, strip):
            front(0, 0)
            strip(0, 0, True)
            with eng.Fori(1, NSTRIP - 1, 2) as i:
                strip(i, 1, True)
                strip(i + 1, 0, True)
            strip(NSTRIP - 1, 1, False)

        NT = TOK // 512
        NS = TOK // 256

        block = ctx.enter_context(nc.Block())

        @block.sync
        def _(sp):
            loads = [(ident[:, :], a["ident"]), (cos[:, :], a["cos"]), (sin[:, :], a["sin"]), (headmask[:, :], a["headmask"]),
                     (sel[:, :], a["sel"]), (onehot_f, a["onehot"]), (decay[:, :], a["decay"]), (decay_q[:, :], a["decay_q"]),
                     (decay_k[:, :], a["decay_k"]), (w_qk[:, :], a["w_qk"]), (w_qk_swap[:, :], a["w_qk_swap"]), (w_v1[:, :], a["w_v1"]),
                     (w_p1[:, :], a["w_p1"]), (w_q2[:, :], a["w_q2"]), (w_k2[:, :], a["w_k2"]), (w_v2[:, :], a["w_v2"]),
                     (w_p2[:, :], a["w_p2"]), (temp[:, :], a["temp"].broadcast_to((C, 1))), (w_i[:, :], a["w_i"]),
                     (shared[:, :, :], a["shared"]), (w_o[:, :], a["w_o"]), (b_o[:, :], a["b_o"]),
                     (w_q3[:, :], a["w_q3"]), (w_k3[:, :], a["w_k3"]), (w_kv3[:, :], a["w_kv3"]), (w_gate[:, :], a["w_gate"]),
                     (w_bin[:, :], a["w_bin"]), (pair_f[:, :], a["pair"]), (scale_bc[:, :], a["scale"].broadcast_to((P, C))),
                     (route_i[:, :], a["route"]), (keep[:, :], a["keep"]), (experts[:, :, 0:NEXP, :], a["experts"])]
            for stage in (T1, T2, L, FF, RT, BN):
                for signal in stage.values():
                    sp.sem_inc(signal, 1)
            for dst, src in loads:
                sp.dma_start(dst, src).then_inc(s_w, 16)
            assert len(loads) == NLOADS
            with sp.Fori(0, NT) as i:
                sp.wait_ge(T1["xT_ps"], times(i))
                sp.dma_start(xin[:, :, :], x_v[:, bass.ds(i * 4, 4), :]).then_inc(T1["x_in"], 16)
                sp.wait_ge(T1["rope"], times((i + 1) * 3))
                sp.wait_ge(T1["scores"], times(i * TOKC["ng"]))
                for n in range(NH):
                    sp.dma_start(q_blocks[n * HD:(n + 1) * HD, :, n, :],
                                 rot[C + n * HD:C + (n + 1) * HD, :].rearrange("d (p q) -> d p q", q=NQ)).then_inc(T1["q_in"], 16)
            sp.wait_ge(s_const, NCONST)
            for b in range(B):
                for j in range(2):
                    for at in (0, (PW - HALF) * PW):
                        sp.dma_start(kx_d[b, j, :, at:at + HALF * PW], zeros[:, :]).then_inc(L["padded"], 16)
            with sp.Fori(0, B) as b:
                with sp.Fori(0, WIN) as w:
                    i = b * WIN + w
                    dst = kx_d.rearrange("b j c n -> (b j) c n")
                    sp.wait_ge(L["xT_sb"], times(i + 1 + 1))
                    settle(sp)
                    sp.wait_ge(L["k_sb"], times(i + 1))
                    settle(sp)
                    sp.wait_ge(L["q_sb"], times((i + 1) * 2))
                    settle(sp)
                    sp.dma_start(dst[bass.ds(b * 2 + 1, 1), :, bass.ds((w * WIN + HALF) * PW, WIN * PW)].rearrange("a c n -> (a c) n"),
                                 xpad[0:C, :]).then_inc(L["stored"], 16)
                    sp.dma_start(dst[bass.ds(b * 2, 1), :, bass.ds((w * WIN + HALF) * PW, WIN * PW)].rearrange("a c n -> (a c) n"),
                                 kpad[:, :]).then_inc(L["stored"], 16)
                    sp.dma_start(qs_d[:, bass.ds(i * 512, 512)], q_sb[:, :]).then_inc(L["stored"], 16)
            sp.wait_ge(L["stored"], times(48 * NT))
            sp.wait_ge(L["padded"], times(16 * 4 * B))
            sp.wait_ge(T1["scores"], times(NT * TOKC["ng"]))
            for par in range(2):
                sp.dma_start(q_half[par][C:KL, :], a["qaug"]).then_inc(T2["q_in"], 16)
            def strip_in(b, s, par):
                i = b * STRIPS + s
                src = kx_d.rearrange("b j c n -> (b j) c n")
                sp.wait_ge(T2["x_patch"], times(i))
                settle(sp)
                sp.dma_start(xst[:, :], src[bass.ds(b * 2 + 1, 1), :, bass.ds(s * (QP * PW), KS * PW)].rearrange("a c n -> (a c) n")).then_inc(T2["k_in"], 16)
                sp.wait_ge(T2["k_patch"], times(i))
                settle(sp)
                sp.dma_start(kst[0:C, :], src[bass.ds(b * 2, 1), :, bass.ds(s * (QP * PW), KS * PW)].rearrange("a c n -> (a c) n")).then_inc(T2["k_in"], 16)
                sp.dma_start(kst[C:KL, :], a["kaug"][bass.ds(s, 1), :, :].rearrange("a c n -> (a c) n")).then_inc(T2["k_in"], 16)
                sp.wait_ge(T2["scores"], times(i * LOCC["ng"]))
                sp.wait_ge(T2["q_in"], times(i * 16 * NH + 32))
                for n in range(NH):
                    sp.dma_start(q_blocks[n * HD:(n + 1) * HD, 16 * par:16 * par + 16, n, :],
                                 qs_d[n * HD:(n + 1) * HD, bass.ds(i * 256, 256)].rearrange("d (p q) -> d p q", q=NQ)).then_inc(T2["q_in"], 16)

            with sp.Fori(0, B) as b:
                with sp.Fori(0, STRIPS // 2) as pair:
                    strip_in(b, pair * 2, 0)
                    strip_in(b, pair * 2 + 1, 1)
            sp.wait_ge(s_prep, 2)
            sp.wait_ge(s_route, 4)
            sp.wait_ge(s_parts, 5)
            for k in range(3):
                for g in range(NG):
                    r = P // NG
                    sp.dma_start(w_parts[k * NG + g:k * NG + g + 1, :].rearrange("a (r n) -> a r n", r=r), w_3[g * r:(g + 1) * r, k:k + 1, :]).then_inc(s_moved, 16)

            def weights_in(i):
                sp.wait_ge(FF["hid_sb"], times(i * 3))
                settle(sp)
                e = sp.value_load(route_x[0:1, bass.ds(i, 1)], min_val=0, max_val=NEXP)
                sp.dma_start(w_exp[:, :, :], experts[:, :, bass.ds(e, 1), :].rearrange("p l a n -> p l (a n)")).then_inc(FF["w_in"], 16)

            def store(i):
                sp.wait_ge(BN["y"], times(i + 1))
                settle(sp)
                sp.dma_start(o_v[:, bass.ds(i * 2, 2), :], yo[:, :, :]).then_inc(BN["stored"], 16)

            def stores(j):
                if not isinstance(j, int) or j < NS:
                    weights_in(j)
                if not isinstance(j, int) or j >= 4:
                    store(j - 4)

            for j in range(4):
                stores(j)
            with sp.Fori(4, NS) as j:
                stores(j)
            for j in range(NS, NS + 4):
                stores(j)
            sp.wait_ge(BN["stored"], times(16 * NS))

        @block.gpsimd
        def _(gp):
            fills = [(xT[:, :], 0.0), (aT[:, :], 0.0), (xnT[0][:, :], 0.0), (xnT[1][:, :], 0.0), (xnT[2][:, :], 0.0), (xT[C:C + 1, :], 1.0), (aT[C:C + 1, :], 1.0), (xnT[0][C:C + 1, :], 1.0), (xnT[1][C:C + 1, :], 1.0), (xnT[2][C:C + 1, :], 1.0),
                     (ones_row[:, :], 0.0), (ones_row[0:1, :], 1.0), (minus_half[:, :], -0.5), (zeros[:, :], 0.0), (xpad[:, :], 0.0),
                     (kpad[:, :], 0.0), (vsb[:, :, :, :], 0.0), (vsb[:, :, :, C:C + 1], 1.0), (qexp[:, :], 0.0), (onehot[:, :], 0.0),
                     (kpatch[:, :, :], 0.0), (xpatch[:, :, :], 0.0), (prob[:, :, :], 0.0), (qk3[:, :], 0.0), (qd3[:, :], 0.0), (state[:, :, :], 0.0),
                     (g3[:, :, :], 0.0), (w_parts[:, :], 0.0), (m_sb[:, :], 0.0), (experts[:, :, NEXP:NEXP + 1, :], 0.0)]
            assert len(fills) == NCONST
            for n, (dst, value) in enumerate(fills):
                if n:
                    gp.wait_ge(s_const, n)
                gp.memset(dst, value).then_inc(s_const, 1)
            gp.wait_ge(s_const, NCONST)
            def patches(buf, n):
                v = buf[0:n, :]
                return bass.AP(v.tensor, v.offset, [list(v.ap[0]), [QP, 16], [PW, KS], [1, KS]])

            def inv_std(name, q, i, after):
                _, _, veps, rstd = ln_sb[name]
                gp.wait_ge(after[0], times(*after[1:]))
                gp.wait_ge(q["veps"], times(i + 1))
                gp.tensor_tensor(rstd[:, :], veps[:, :], minus_half[:, 0:veps.shape[1]], ALU.pow).then_inc(q["rstd"], 1)

            with gp.Fori(0, NT) as i:
                inv_std("pre", L, i, (L["rstd"], i))
            def strip_patches(i, par):
                gp.wait_ge(T2["k_in"], times((i + 1) * 48))
                gp.wait_ge(T2["k_patch"], times(i))
                gp.wait_ge(T2["v_ps"], times(i * 2))
                settle(gp)
                gp.tensor_copy(xpatch[0:C, par, :].rearrange("c (p r w) -> c p r w", p=16, r=KS), patches(xst, C)).then_inc(T2["x_patch"], 1)
                gp.wait_ge(T2["scores"], times(i * LOCC["ng"]))
                settle(gp)
                gp.wait_ge(T2["x_patch"], times(i + 1))
                settle(gp)
                gp.tensor_copy(kpatch[0:KL, par, :].rearrange("c (p r w) -> c p r w", p=16, r=KS), patches(kst, KL)).then_inc(T2["k_patch"], 1)

            with gp.Fori(0, NS, 2) as i:
                strip_patches(i, 0)
                strip_patches(i + 1, 1)

            def inv_stds(j):
                if not isinstance(j, int) or j < NS:
                    inv_std("ffn", FF, j, (BN["rstd"], j - 2))
                if not isinstance(j, int) or 1 <= j < NS + 1:
                    inv_std("ret", RT, j - 1, (FF["rstd"], j + 1, NS))
                if not isinstance(j, int) or j >= 2:
                    inv_std("bin", BN, j - 2, (RT["rstd"], j, NS))

            for j in range(2):
                inv_stds(j)
            with gp.Fori(2, NS) as j:
                inv_stds(j)
            for j in range(NS, NS + 2):
                inv_stds(j)

        @block.tensor
        def _(pe):
            def peak(c, i, par, g):
                q, nk, ng = c["s"], c["nk"], c["ng"]
                pe.wait_ge(q["max_done"], times(i * ng + g))
                for u in range(GP):
                    mm = pe.matmul(bank["MX"][:, u * nk:(u + 1) * nk], c["q"](par, g * GP + u, True), c["k"](par, g * GP + u, True),
                                   start=True, stop=True)
                mm.then_inc(q["max_scores"], 1)

            def turn_maxima(c, i):
                q = c["s"]
                pe.wait_ge(q["max_done"], times((i + 1) * c["ng"]))
                pe.wait_ge(q["negmax"], times(i))
                pe.transpose(bank["T"][:, 0:P], m_sb[:, :], ident[:, :]).then_inc(q["maxT"], 1)

            def attention(c, i, par, between=lambda g: None):
                q, nk, ng = c["s"], c["nk"], c["ng"]
                pe.wait_ge(q["negmax"], times(i + 1))

                def scores(g):
                    pe.wait_ge(q["exp_done"], times(i * ng + g + 1))
                    settle(pe)
                    for u in range(GP):
                        o = S[g % 2][0:nk, u * P:(u + 1) * P]
                        pe.matmul(o, c["k"](par, g * GP + u, False), c["q"](par, g * GP + u, False), start=True, stop=False)
                        mm = pe.matmul(o, onehot_v[:, g * GP + u, 0:nk], mT[:, par, :], start=False, stop=True)
                    mm.then_inc(q["scores"], 1)

                def values(g):
                    pe.wait_ge(q["exp_done"], times(i * ng + g + 3))
                    pe.wait_ge(q["norm_done"], times((i * ng + g) * 2))
                    for u in range(GP):
                        mm = pe.matmul(bank["AV"][:, u * P:(u + 1) * P], prob[0:c["kv"], g % 2, u * P:(u + 1) * P],
                                       c["v"](par, g * GP + u), start=True, stop=True)
                    mm.then_inc(q["av_done"], 1)

                def select(g):
                    pe.wait_ge(q["norm_done"], times((i * ng + g + 1) * 2))
                    if g == 0:
                        pe.wait_ge(q["attn_out"], times(i))
                        settle(pe)
                    for u in range(GP):
                        p = g * GP + u
                        r, w = c["at"](p)
                        o = bank["OT"][0:C, :].rearrange("c (r w) -> c r w", w=W)[:, r:r + QP, w:w + QP]
                        mm = pe.matmul(o, msk[:, g % 2, u * C:(u + 1) * C], selr[:, g % 2, u * NQ:(u + 1) * NQ], start=True, stop=True)
                    mm.then_inc(q["sel_done"], 1)

                for g in range(ng + 2):
                    if g < ng:
                        scores(g)
                    between(g)
                    if 1 <= g <= ng:
                        if g == 1:
                            pe.wait_ge(q["v_sb"], times((i + 1) * c["nv"]))
                        values(g - 1)
                    if g >= 2:
                        select(g - 2)

            def project(q, i, n, w):
                pe.wait_ge(q["attn_out"], times(i + 1))
                pe.wait_ge(q["h_done"], times(i))
                for t in range(n):
                    mm = pe.matmul(bank["J2"][:, t * C:(t + 1) * C], aT[:, t * P:(t + 1) * P], w[:, :], start=True, stop=True)
                mm.then_inc(q["proj"], 1)

            def turn(src, width, n, q, k):
                settle(pe)
                for t in range(n):
                    mm = pe.transpose(bank["T"][0:width, t * P:(t + 1) * P], src(t), ident[:, :])
                mm.then_inc(q[k], 1)

            pe.wait_ge(s_w, 16 * NLOADS)
            pe.wait_ge(s_const, NCONST)
            pe.wait_ge(s_prep, 3)
            with pe.Fori(0, NT) as i:
                pe.wait_ge(T1["x_in"], times((i + 1) * 16))
                pe.wait_ge(T1["negmax"], times(i))
                turn(lambda t: xin[:, t, :], C, 4, T1, "xT_ps")
                pe.wait_ge(T1["xT_sb"], times(i + 1))
                pe.wait_ge(T1["h_done"], times(i))
                pe.matmul(bank["J1"][:, :], w_qk[:, :], xT[:, :], start=True, stop=True)
                pe.matmul(bank["J2"][:, :], w_qk_swap[:, :], xT[:, :], start=True, stop=True).then_inc(T1["qk_ps"], 1)
                pe.wait_ge(T1["attn_out"], times(i))
                for n in range(8):
                    mm = pe.matmul(bank["OT"][0:NKT, n * C:(n + 1) * C], xT[:, n * NKT:(n + 1) * NKT], w_v1[:, :], start=True, stop=True)
                mm.then_inc(T1["v_ps"], 1)
                pe.wait_ge(T1["v_sb"], times(i + 1))
                pe.wait_ge(T1["q_in"], times((i + 1) * 16 * NH))
                pe.wait_ge(T1["rope"], times((i + 1) * 3))
                for g in range(TOKC["ng"]):
                    peak(TOKC, i, 0, g)
                turn_maxima(TOKC, i)
                attention(TOKC, i, 0)
                project(T1, i, 4, w_p1)
            with pe.Fori(0, NT) as i:
                pe.wait_ge(L["xn"], times((i + 1) * 4))
                turn(lambda t: xn[:, t, :], C, 4, L, "xT_ps")
                pe.wait_ge(L["xT_sb"], times(i + 2))
                pe.wait_ge(L["k_sb"], times(i))
                pe.wait_ge(L["q_sb"], times(i * 2))
                xw = xpad[:, :].rearrange("c (r w) -> c r w", w=PW)[:, :, HALF:HALF + W]
                settle(pe)
                pe.matmul(bank["J1"][0:C, :], w_k2[:, :], xw, start=True, stop=True).then_inc(L["k_ps"], 1)
                pe.matmul(bank["J2"][0:C, :], w_q2[:, :], xw, start=True, stop=True).then_inc(L["q_ps"], 1)
            pe.sem_inc(T2["scores"], LOCC["credit"])
            pe.sem_inc(T2["v_ps"], 2)

            def local_values(i, par, hf):
                pe.wait_ge(T2["x_patch"], times(i + 1))
                pe.wait_ge(T2["v_sb"], times(i * 2 + hf))
                settle(pe)
                for u in range(8):
                    p = hf * 8 + u
                    mm = pe.matmul(bank["J1"][0:NKL, u * C:(u + 1) * C], xpatch[:, par, p * NKL:(p + 1) * NKL], w_v2[:, :], start=True, stop=True)
                mm.then_inc(T2["v_ps"], 1)

            def front_part(i, par, g):
                if g in (0, 2):
                    local_values(i, par, g // 2)
                if g == 0:
                    pe.wait_ge(T2["k_patch"], times(i + 1))
                    pe.wait_ge(T2["q_in"], times((i + 1) * 16 * NH + 32))
                if g < LOCC["ng"]:
                    peak(LOCC, i, par, g)
                if g == LOCC["ng"]:
                    turn_maxima(LOCC, i)

            def front(i, par):
                for g in range(LOCC["ng"] + 1):
                    front_part(i, par, g)

            def strip(i, par, more):
                def between(g):
                    if more:
                        front_part(i + 1, 1 - par, g)
                    if g == 1 and not (isinstance(i, int) and i == 0):
                        project(T2, i - 1, 2, w_p2)
                attention(LOCC, i, par, between)

            strips_ahead(pe, front, strip)
            project(T2, NS - 1, 2, w_p2)
            pe.wait_ge(s_moved, 16 * 3 * NG + 2)

            def strips(j, par):
                f, r, g, q = (inside(j - k) for k in range(4))

                def weights(q, k, half):
                    pe.wait_ge(BN["sign"], times(q * 8 + k + 1))
                    for u in range(4):
                        mm = pe.matmul(double[k % 2][:, u * 256:(u + 1) * 256],
                                       w_parts[:, (k * 4 + u) * P:(k * 4 + u + 1) * P], g3[:, half, :], start=True, stop=True)
                    mm.then_inc(BN["w_ps"], 1)

                def reduce(k):
                    if k == 0:
                        pe.wait_ge(BN["y_scaled"], times(q))
                    pe.wait_ge(BN["prod"], times(q * 8 + k + 1))
                    for u in range(4):
                        for t in range(2):
                            mm = pe.matmul(bank["AV"][:, t * C + (k * 4 + u) * 2:t * C + (k * 4 + u) * 2 + 2],
                                           prod[:, k % 2, u * 256 + t * P:u * 256 + (t + 1) * P], pair_sel[:, :], start=True, stop=True)
                    mm.then_inc(BN["y_part"], 1)

                for k in range(8):
                    if k < 7 and q is not None:
                        weights(q, k + 1, 1 - par)
                    if k == 7 and g is not None:
                        pe.wait_ge(BN["gates"], times(g + 1))
                        weights(g, 0, par)
                    if k and q is not None:
                        reduce(k - 1)
                    if k == 0 and f is not None:
                        pe.wait_ge(FF["xn"], times((f + 1) * 2))
                        pe.wait_ge(RT["state"], times((f - 1) * 2, 2 * NS))
                        turn(lambda t: xn_f[:, t, :], C, 2, FF, "xT_ps")
                    if k == 1:
                        if f is not None:
                            pe.wait_ge(FF["xT_sb"], times(f + 1))
                            pe.wait_ge(FF["h_done"], times(f))
                            pe.matmul(bank["J1"][:, 0:256], w_i[:, :], xnT[0][:, :], start=True, stop=True).then_inc(FF["hid_ps"], 1)
                        if r is not None:
                            pe.wait_ge(RT["xn"], times((r + 1) * 2))
                            pe.wait_ge(FF["xT_sb"], times(r + 2, NS))
                            turn(lambda t: xn_r[:, t, :], C, 2, RT, "xT_ps")
                    if k == 2:
                        if f is not None:
                            pe.wait_ge(FF["w_in"], times((f + 1) * 16))
                            pe.wait_ge(FF["hid_sb"], times(f * 3 + 1))
                            pe.matmul(bank["J1"][:, 0:256], w_exp[:, 0, 0:HID], hidT[:, 0, :], start=True, stop=True).then_inc(FF["hid_ps"], 1)
                        if g is not None:
                            pe.wait_ge(BN["xn"], times((g + 1) * 2))
                            pe.wait_ge(RT["xT_sb"], times(g + 2, NS))
                            turn(lambda t: xn2[:, t, :, :], P, 2, BN, "xT_ps")
                        if r is not None:
                            pe.wait_ge(RT["xT_sb"], times(r + 1))
                            pe.wait_ge(RT["h_done"], times(r))
                            settle(pe)
                            pe.matmul(bank["OT"][0:C, 0:256], w_q3[:, :], xnT[1][:, :], start=True, stop=True)
                            pe.matmul(bank["OT"][0:C, 256:512], w_k3[:, :], xnT[1][:, :], start=True, stop=True).then_inc(RT["qk_ps"], 1)
                    if k == 3:
                        if g is not None:
                            pe.wait_ge(BN["xT_sb"], times(g + 1))
                            pe.wait_ge(FF["hid_sb"], times(g * 3 + 8, 3 * NS))
                            settle(pe)
                            pe.matmul(bank["J1"][0:3 * NG, 0:256], w_gate[:, :], xnT[2][:, :], start=True, stop=True).then_inc(BN["g_ps"], 1)
                        if r is not None:
                            pe.wait_ge(BN["xb"], times(r))
                            pe.wait_ge(BN["xT_sb"], times(r))
                            for t in range(2):
                                mm = pe.matmul(bank["T"][:, t * P:(t + 1) * P], xnT[1][:, t * P:(t + 1) * P], w_kv3[:, :], start=True, stop=True)
                            mm.then_inc(RT["kv_ps"], 1)
                        if f is not None:
                            pe.wait_ge(FF["hid_sb"], times(f * 3 + 2))
                            pe.wait_ge(BN["gates"], times(f - 1))
                            pe.matmul(bank["J1"][:, 0:256], w_exp[:, 1, 0:HID], hidT[:, 1, :], start=True, stop=True).then_inc(FF["hid_ps"], 1)
                    if k == 4:
                        if r is not None:
                            pe.wait_ge(RT["qk_sb"], times(r + 1))
                            for t in range(2):
                                mm = pe.matmul(bank["OT"][:, t * P:(t + 1) * P], qk3[:, 256 + t * P:256 + (t + 1) * P], qk3[:, t * P:(t + 1) * P],
                                               start=True, stop=True)
                            mm.then_inc(RT["s_ps"], 1)
                        if f is not None:
                            pe.wait_ge(FF["hid_sb"], times(f * 3 + 3))
                            for t in range(2):
                                pe.matmul(bank["J1"][:, t * C:(t + 1) * C], hidT[:, 2, t * P:(t + 1) * P], w_o[:, :], start=True, stop=False)
                                mm = pe.matmul(bank["J1"][:, t * C:(t + 1) * C], ones_row[:, :], b_o[:, :], start=False, stop=True)
                            mm.then_inc(FF["out_ps"], 1)
                    if k == 6 and r is not None:
                        pe.wait_ge(RT["kd"], times(r + 1))
                        pe.wait_ge(RT["v"], times(r + 1))
                        pe.wait_ge(RT["sd"], times(r + 1))
                        pe.wait_ge(RT["qd"], times(r + 1))
                        pe.wait_ge(RT["reset"], times(r + 1))
                        for t in range(2):
                            if t:
                                pe.wait_ge(RT["state"], times(r * 2 + 1))
                                settle(pe)
                            pe.matmul(bank["T"][0:C, 0:C], kd3[:, t, :], v3[:, t, :], start=True, stop=True).then_inc(RT["kv_sum"], 1)
                            pe.matmul(bank["OT"][:, t * C:(t + 1) * C], sd3[:, t, :], v3[:, t, :], start=True, stop=False)
                            mm = pe.matmul(bank["OT"][:, t * C:(t + 1) * C], qd3[:, t * P:(t + 1) * P], state[:, t, :], start=False, stop=True)
                        mm.then_inc(RT["out_ps"], 1)
                if q is not None:
                    reduce(7)

            staggered(pe, strips)

        @block.scalar
        def _(act):
            def neg_max(c, i, par):
                q = c["s"]
                act.wait_ge(q["maxT"], times(i + 1))
                act.wait_ge(q["scores"], times(i * c["ng"]))
                act.activation(mT[:, par, :], bank["T"][:, 0:P], ACT.Copy, scale=-1.0).then_inc(q["negmax"], 1)

            def attention(c, i, between=lambda g: None):
                q, nk, ng = c["s"], c["nk"], c["ng"]
                for g in range(ng):
                    act.wait_ge(q["scores"], times(i * ng + g + 1 + c["credit"]))
                    act.wait_ge(q["av_done"], times(i * ng + g + 1))
                    act.activation(prob[0:nk, g % 2, :], S[g % 2][0:nk, :], ACT.Exp).then_inc(q["exp_done"], 1)
                    between(g)
                act.wait_ge(q["sel_done"], times((i + 1) * ng + 2))
                act.wait_ge(q["proj"], times(i))
                n = c["np"] * NQ
                act.activation(aT[0:C, 0:n], bank["OT"][0:C, 0:n], ACT.Copy).then_inc(q["attn_out"], 1)

            act.wait_ge(s_w, 16 * NLOADS)
            act.wait_ge(s_const, NCONST)
            act.activation(rstd_warm[:, :], ident[:, 0:1], ACT.Exp)
            act.sem_inc(T1["exp_done"], 2)
            act.sem_inc(T2["exp_done"], 2)
            act.sem_inc(BN["sign"], 2)
            act.sem_inc(L["xT_sb"], 1)
            with act.Fori(0, NT) as i:
                act.wait_ge(T1["xT_ps"], times(i + 1))
                act.activation(xT[0:C, :].rearrange("c (n r w) -> c n r w", n=8, r=WIN),
                               bank["T"][0:C, :].rearrange("c (r n w) -> c n r w", n=8, r=WIN), ACT.Copy).then_inc(T1["xT_sb"], 1)
                act.wait_ge(T1["v_ps"], times(i + 1))
                act.activation(vsb[0:NKT, 0, 0:8, 0:C], bank["OT"][0:NKT, :].rearrange("p (n c) -> p n c", c=C), ACT.Copy).then_inc(T1["v_sb"], 1)
                act.wait_ge(T1["maxT"], times(i + 1))
                act.activation(mT[:, 0, :], bank["T"][:, 0:P], ACT.Copy, scale=-1.0).then_inc(T1["negmax"], 1)
                attention(TOKC, i)
            with act.Fori(0, NT) as i:
                act.wait_ge(L["xT_ps"], times(i + 1))
                act.wait_ge(L["stored"], times(i * 48))
                act.activation(xpad[0:C, :].rearrange("c (r w) -> c r w", w=PW)[:, :, HALF:HALF + W],
                               bank["T"][0:C, :].rearrange("c (r w) -> c r w", w=W), ACT.Copy).then_inc(L["xT_sb"], 1)
                act.wait_ge(L["k_ps"], times(i + 1))
                act.activation(kpad[:, :].rearrange("c (r w) -> c r w", w=PW)[:, :, HALF:HALF + W],
                               bank["J1"][0:C, :].rearrange("c (r w) -> c r w", w=W), ACT.Copy).then_inc(L["k_sb"], 1)
            def local_values(i, par, hf):
                act.wait_ge(T2["v_ps"], times(i * 2 + hf + 1 + 2))
                act.wait_ge(T2["av_done"], times((i - 1) * LOCC["ng"] + 2))
                act.activation(vsb[0:NKL, par, hf * 8:hf * 8 + 8, 0:C], bank["J1"][0:NKL, :].rearrange("p (n c) -> p n c", c=C), ACT.Copy).then_inc(T2["v_sb"], 1)

            def front(i, par):
                for hf in range(2):
                    local_values(i, par, hf)
                neg_max(LOCC, i, par)

            def strip(i, par, more):
                def between(g):
                    if more and g in (0, 2):
                        local_values(i + 1, 1 - par, g // 2)
                    if more and g == LOCC["ng"] - 1:
                        neg_max(LOCC, i + 1, 1 - par)
                attention(LOCC, i, between)

            strips_ahead(act, front, strip)

            def strips(j, par):
                f, r, g, q = (inside(j - k) for k in range(4))
                for k in range(8):
                    if q is not None:
                        act.wait_ge(BN["w_ps"], times(q * 8 + k + 1))
                        act.wait_ge(BN["prod"], times(q * 8 + k - 1))
                        act.activation(sgn[:, k % 2, :], double[k % 2][:, :], ACT.Sign).then_inc(BN["sign"], 1)
                    if k == 1:
                        if f is not None:
                            act.wait_ge(FF["xT_ps"], times(f + 1))
                            act.activation(xnT[0][0:C, :], bank["T"][0:C, 0:256], ACT.Copy).then_inc(FF["xT_sb"], 1)
                    if k == 2:
                        if f is not None:
                            act.wait_ge(FF["hid_ps"], times(f * 3 + 1))
                            act.wait_ge(FF["out_ps"], times(f))
                            act.activation(hidT[:, 0, :], bank["J1"][:, 0:256], ACT.Relu).then_inc(FF["hid_sb"], 1)
                        if r is not None:
                            act.wait_ge(RT["xT_ps"], times(r + 1))
                            act.activation(xnT[1][0:C, :], bank["T"][0:C, 0:256], ACT.Copy).then_inc(RT["xT_sb"], 1)
                    if k == 3:
                        if f is not None:
                            act.wait_ge(FF["hid_ps"], times(f * 3 + 2))
                            act.activation(hidT[:, 1, :], bank["J1"][:, 0:256], ACT.Relu, bias=w_exp[:, 0, HID:HID + 1]).then_inc(FF["hid_sb"], 1)
                        if g is not None:
                            act.wait_ge(BN["xT_ps"], times(g + 1))
                            act.wait_ge(BN["prod"], times((g - 1) * 8))
                            act.activation(xnT[2][0:C, :], bank["T"][0:C, 0:256], ACT.Copy).then_inc(BN["xT_sb"], 1)
                            act.activation(xb2[:, par, :], bank["T"][:, 0:256], ACT.Sign).then_inc(BN["xb"], 1)
                        if r is not None:
                            act.wait_ge(RT["qk_ps"], times(r + 1))
                            act.activation(qk3[0:C, :], bank["OT"][0:C, :], ACT.Copy).then_inc(RT["qk_sb"], 1)
                    if k == 4:
                        if f is not None:
                            act.wait_ge(FF["hid_ps"], times(f * 3 + 3))
                            act.activation(hidT[:, 2, :], bank["J1"][:, 0:256], ACT.Relu, bias=w_exp[:, 1, HID:HID + 1]).then_inc(FF["hid_sb"], 1)
                        if r is not None:
                            act.wait_ge(RT["kv_ps"], times(r + 1))
                            act.wait_ge(RT["kd"], times(r + 1))
                            act.activation(v3[:, :, :], bank["T"][:, 0:256].rearrange("p (t n) -> p t n", t=2)[:, :, C:2 * C], ACT.Copy).then_inc(RT["v"], 1)

            staggered(act, strips)

        @block.vector
        def _(dve):
            def maxima(c, i, g):
                q, nk, ng = c["s"], c["nk"], c["ng"]
                dve.wait_ge(q["maxT"], times(i))
                dve.wait_ge(q["max_scores"], times(i * ng + g + 1))
                dve.tensor_reduce(m_sb[:, g * GP:(g + 1) * GP], bank["MX"][:, 0:GP * nk].rearrange("p (u n) -> p u n", u=GP),
                                  AX.X, ALU.max).then_inc(q["max_done"], 1)

            def weigh(c, i, g):
                q, ng = c["s"], c["ng"]
                v = bank["AV"][:, :].rearrange("p (u n) -> p u n", u=GP)
                dve.wait_ge(q["av_done"], times(i * ng + g + 3))
                dve.wait_ge(q["sel_done"], times(i * ng + g + 1))
                dve.reciprocal(rec[:, g % 2, :], v[:, :, C]).then_inc(q["rec_done"], 1)
                dve.tensor_tensor(msk[:, g % 2, :].rearrange("p (u n) -> p u n", u=GP), v[:, :, 0:C],
                                  headmask[:, :].rearrange("p (a n) -> p a n", a=1).broadcast_to((P, GP, C)), ALU.mult).then_inc(q["norm_done"], 1)
                dve.wait_ge(q["rec_done"], times(i * ng + g + 1))
                dve.tensor_tensor(selr[:, g % 2, :].rearrange("p (u n) -> p u n", u=GP),
                                  sel[:, :].rearrange("p (a n) -> p a n", a=1).broadcast_to((P, GP, NQ)),
                                  rec[:, g % 2, :].rearrange("p (u a) -> p u a", a=1).broadcast_to((P, GP, NQ)), ALU.mult).then_inc(q["norm_done"], 1)

            def moments(name, q, i, src):
                stats, mv, veps, _ = ln_sb[name]
                n = stats.shape[1]
                for t in range(n):
                    dve.bn_stats(stats[:, t, :], src(t)).then_inc(q["stats"], 1)
                for t in range(n):
                    dve.wait_ge(q["stats"], times(i * n + t + 1))
                    settle(dve)
                    dve.bn_aggr(mv[:, t, :], stats[:, t, :]).then_inc(q["mv"], 1)
                dve.wait_ge(q["mv"], times((i + 1) * n))
                dve.tensor_scalar(veps[:, :], mv[:, :, 1], EPS, None, ALU.add).then_inc(q["veps"], 1)

            def normalize(name, q, i, src, dst):
                _, mv, _, rstd = ln_sb[name]
                dve.wait_ge(q["rstd"], times(i + 1))
                dve.wait_ge(q["xT_ps"], times(i))
                for t in range(mv.shape[1]):
                    s = src(t)
                    d = dst(t)
                    if len(d.shape) == 3:
                        s = s.rearrange("p (a c) -> p a c", a=1).broadcast_to((P, 2, C))
                    dve.tensor_scalar(d, s, mv[:, t, 0:1], rstd[:, t:t + 1], ALU.subtract, ALU.mult).then_inc(q["xn"], 1)

            def rows(t0, n):
                return h[:, bass.ds(t0, n), :]

            def row(t0):
                return lambda t: h[:, bass.ds(t0 + t, 1), :].rearrange("p a c -> p (a c)")

            dve.sem_inc(T1["av_done"], 2)
            dve.sem_inc(T2["av_done"], 2)
            dve.sem_inc(T1["sel_done"], 2)
            dve.sem_inc(T2["sel_done"], 2)
            dve.wait_ge(s_w, 16 * NLOADS)
            dve.wait_ge(s_const, NCONST)
            dve.tensor_copy(route_f[:, :], route_i[:, :]).then_inc(s_parts, 1)
            dve.tensor_copy(onehot[0:32, :], onehot_f).then_inc(s_prep, 1)
            dve.tensor_tensor(shared[:, :, 0:HID], shared[:, :, 0:HID],
                              ident[:, :].rearrange("p (a n) -> p a n", a=1).broadcast_to((P, NLAY, P)), ALU.add).then_inc(s_route, 1)
            dve.wait_ge(s_route, 1)
            for l in range(NLAY):
                dve.tensor_tensor(experts[:, l, :, :], experts[:, l, :, :],
                                  shared[:, l, :].rearrange("p (a n) -> p a n", a=1).broadcast_to((P, NEXP + 1, HID + 1)), ALU.add).then_inc(s_prep, 1)
            dve.tensor_scalar(route_ok[:, :], route_i[:, :], 0.0, None, ALU.is_ge).then_inc(s_route, 1)
            dve.wait_ge(s_route, 2)
            dve.scalar_tensor_tensor(out=route_ok[:, :], in0=route_i[:, :], scalar=float(NEXP), in1=route_ok[:, :], op0=ALU.is_lt, op1=ALU.mult).then_inc(s_route, 1)
            dve.wait_ge(s_route, 3)
            dve.scalar_tensor_tensor(out=route_f[:, :], in0=route_i[:, :], scalar=-float(NEXP), in1=route_ok[:, :], op0=ALU.add, op1=ALU.mult).then_inc(s_parts, 1)
            dve.wait_ge(s_parts, 2)
            dve.tensor_scalar(route_x[:, :], route_f[:, :], float(NEXP), None, ALU.add).then_inc(s_route, 1)
            dve.tensor_copy(w_3[:, 0, :], w_bin[:, :]).then_inc(s_parts, 1)
            dve.wait_ge(s_parts, 3)
            dve.tensor_tensor(w_rest[:, :], w_bin[:, :], w_3[:, 0, :], ALU.subtract).then_inc(s_moved, 1)
            dve.wait_ge(s_moved, 1)
            dve.tensor_copy(w_3[:, 1, :], w_rest[:, :]).then_inc(s_parts, 1)
            dve.wait_ge(s_parts, 4)
            dve.tensor_tensor(w_3[:, 2, :], w_rest[:, :], w_3[:, 1, :], ALU.subtract).then_inc(s_parts, 1)
            dve.tensor_copy(pair_sel[:, :], pair_f[:, :]).then_inc(s_moved, 1)

            with dve.Fori(0, NT) as i:
                dve.wait_ge(T1["qk_ps"], times(i + 1))
                dve.wait_ge(T1["q_in"], times(i * 16 * NH))
                dve.tensor_tensor(t_cos[:, :], bank["J1"][:, :], cos[:, :], ALU.mult).then_inc(T1["rope_mul"], 1)
                dve.tensor_tensor(t_sin[:, :], bank["J2"][:, :], sin[:, :], ALU.mult).then_inc(T1["rope_mul"], 1)
                dve.wait_ge(T1["rope_mul"], times((i + 1) * 2))
                dve.wait_ge(T1["scores"], times(i * TOKC["ng"]))
                dve.tensor_tensor(rot[0:C, :], t_cos[0:C, :], t_sin[0:C, :], ALU.add).then_inc(T1["rope"], 1)
                for pc in range(2):
                    def half(b):
                        return b[C:2 * C, :].rearrange("k (n r p c) -> k p n r c", n=16, r=QP, p=2)[:, pc, :, :, :]
                    dve.tensor_tensor(rot[C:2 * C, :].rearrange("k (n p r c) -> k p n r c", n=16, r=QP, p=2)[:, pc, :, :, :],
                                      half(t_cos), half(t_sin), ALU.add).then_inc(T1["rope"], 1)
                for g in range(TOKC["ng"]):
                    maxima(TOKC, i, g)
                for g in range(TOKC["ng"]):
                    weigh(TOKC, i, g)
                dve.wait_ge(T1["proj"], times(i + 1))
                dve.tensor_copy(rows(i * 4, 4), bank["J2"][:, 0:256].rearrange("p (t c) -> p t c", t=4)).then_inc(T1["h_done"], 1)
            dve.wait_ge(T1["h_done"], times(NT))
            with dve.Fori(0, NT) as i:
                moments("pre", L, i, row(i * 4))
                normalize("pre", L, i, row(i * 4), lambda t: xn[:, t, :])
                dve.wait_ge(L["q_ps"], times(i + 1))
                dve.wait_ge(L["stored"], times(i * 48))
                for t in range(2):
                    dve.tensor_scalar(q_sb[:, t * 256:(t + 1) * 256].rearrange("c (p r w) -> c p r w", p=16, r=QP),
                                      bank["J2"][0:C, t * 256:(t + 1) * 256].rearrange("c (r p w) -> c p r w", p=16, r=QP),
                                      temp[:, :], float(HD ** -0.5), ALU.mult, ALU.mult).then_inc(L["q_sb"], 1)
            def front(i, par):
                for g in range(LOCC["ng"]):
                    maxima(LOCC, i, g)

            def residual(i):
                dve.wait_ge(T2["proj"], times(i + 1))
                dve.tensor_tensor(rows(i * 2, 2), bank["J2"][:, 0:128].rearrange("p (t c) -> p t c", t=2), rows(i * 2, 2), ALU.add).then_inc(T2["h_done"], 1)

            def strip(i, par, more):
                for g in range(LOCC["ng"] + 1):
                    if g < LOCC["ng"] and more:
                        maxima(LOCC, i + 1, g)
                    if g == 1 and not (isinstance(i, int) and i == 0):
                        residual(i - 1)
                    if g:
                        weigh(LOCC, i, g - 1)

            strips_ahead(dve, front, strip)
            residual(NS - 1)
            dve.wait_ge(T2["h_done"], times(NS))

            def add_rows(i, ps, q):
                dve.tensor_tensor(rows(i * 2, 2), bank[ps][:, 0:128].rearrange("p (t c) -> p t c", t=2), rows(i * 2, 2), ALU.add).then_inc(q["h_done"], 1)

            def strips(j, par):
                f, r, g, q = (inside(j - k) for k in range(4))
                if f is not None:
                    moments("ffn", FF, f, row(f * 2))
                for k in range(8):
                    if q is not None:
                        dve.wait_ge(BN["sign"], times(q * 8 + k + 3))
                        dve.wait_ge(BN["y_part"], times(q * 8 + k - 1))
                        dve.tensor_tensor(prod[:, k % 2, :].rearrange("p (u n) -> p u n", u=4), sgn[:, k % 2, :].rearrange("p (u n) -> p u n", u=4),
                                          xb2[:, 1 - par:2 - par, :].broadcast_to((P, 4, 256)), ALU.mult).then_inc(BN["prod"], 1)
                    if k == 0:
                        if f is not None:
                            normalize("ffn", FF, f, row(f * 2), lambda t: xn_f[:, t, :])
                        if r is not None:
                            dve.wait_ge(FF["h_done"], times(r + 1))
                            settle(dve)
                            moments("ret", RT, r, row(r * 2))
                    if k == 1:
                        if r is not None:
                            normalize("ret", RT, r, row(r * 2), lambda t: xn_r[:, t, :])
                            dve.wait_ge(RT["state"], times(r * 2))
                            dve.tensor_scalar(state[0:C, 0, :], state[0:C, 0, :], keep[0:C, bass.ds(r, 1)], None, ALU.mult).then_inc(RT["reset"], 1)
                        if g is not None:
                            dve.wait_ge(RT["h_done"], times(g + 1))
                            settle(dve)
                            moments("bin", BN, g, row(g * 2))
                    if k == 2 and g is not None:
                        normalize("bin", BN, g, row(g * 2), lambda t: xn2[:, t, :, :])
                    if k == 3:
                        if g is not None:
                            dve.wait_ge(BN["g_ps"], times(g + 1))
                            dve.wait_ge(BN["w_ps"], times((g - 1) * 8))
                            dve.tensor_scalar(g3[0:3 * NG, par, :], bank["J1"][0:3 * NG, 0:256], 0.0, None, ALU.is_gt).then_inc(BN["gates"], 1)
                    if k == 4:
                        if r is not None:
                            dve.wait_ge(RT["kv_ps"], times(r + 1))
                            dve.wait_ge(RT["out_ps"], times(r))
                            dve.tensor_scalar(kd3[:, :, :], bank["T"][:, 0:256].rearrange("p (t n) -> p t n", t=2)[:, :, 0:C],
                                              decay_k[:, :], None, ALU.mult).then_inc(RT["kd"], 1)
                            dve.wait_ge(RT["qk_sb"], times(r + 1))
                            dve.tensor_tensor(qd3[0:C, :], qk3[0:C, 0:256], decay_q[:, :], ALU.mult).then_inc(RT["qd"], 1)
                    if k == 5:
                        if r is not None:
                            dve.wait_ge(RT["s_ps"], times(r + 1))
                            dve.tensor_tensor(sd3[:, :, :], bank["OT"][:, 0:256].rearrange("p (t n) -> p t n", t=2),
                                              decay[:, :].rearrange("p (a n) -> p a n", a=1).broadcast_to((P, 2, P)), ALU.mult).then_inc(RT["sd"], 1)
                        if f is not None:
                            dve.wait_ge(FF["out_ps"], times(f + 1))
                            add_rows(f, "J1", FF)
                    if k == 6 and r is not None:
                        for t in range(2):
                            dve.wait_ge(RT["kv_sum"], times(r * 2 + t + 1))
                            dve.wait_ge(RT["reset"], times(r + 1))
                            if t == 1:
                                dve.wait_ge(RT["state"], times(r * 2 + 1))
                                dve.wait_ge(RT["out_ps"], times(r + 1))
                            dve.scalar_tensor_tensor(out=state[0:C, 1 - t, :], in0=state[0:C, t, :], scalar=float(ALPHA ** P),
                                                     in1=bank["T"][0:C, 0:C], op0=ALU.mult, op1=ALU.add).then_inc(RT["state"], 1)
                        add_rows(r, "OT", RT)
                if q is not None:
                    dve.wait_ge(BN["y_part"], times((q + 1) * 8))
                    dve.wait_ge(BN["y"], times(q))
                    dve.tensor_tensor(ys[:, :, :], bank["AV"][:, 0:128].rearrange("p (t c) -> p t c", t=2),
                                      scale_bc[:, :].rearrange("p (a n) -> p a n", a=1).broadcast_to((P, 2, C)), ALU.mult).then_inc(BN["y_scaled"], 1)
                    dve.wait_ge(BN["y_scaled"], times(q + 1))
                    dve.wait_ge(BN["stored"], times(q * 16))
                    dve.tensor_tensor(yo[:, :, :], ys[:, :, :], rows(q * 2, 2), ALU.add).then_inc(BN["y"], 1)

            staggered(dve, strips)


NLOADS = 32
NSTRIP = TOK // 256
NCONST = 30


def _with_bias(w, b):
    return np.concatenate([w, b[None, :]], 0)


def kernel(x, L0_tok_qkv_w, L0_tok_qkv_b, L0_tok_proj_w, L0_tok_proj_b, L0_attn_W_qkv, L0_attn_W_proj, L0_attn_b_proj,
           L0_attn_temperature, L0_ffn_route_id, L0_ffn_Wi, L0_ffn_bi, L0_ffn_Wr, L0_ffn_br, L0_ffn_Ws, L0_ffn_bs, L0_ffn_Wo,
           L0_ffn_bo, L1_attn_Wqkv, L1_attn_bqkv, L1_ffn_weight, L1_ffn_proj_w, L1_ffn_proj_b, L1_ffn_scale):
    import concourse.bacc as _bacc
    from concourse.bass_utils import run_bass_kernel_spmd as _run

    n = np.asarray
    arr = {k: v for k, v in shape_tables().items()}
    arr["pair"] = (np.arange(P)[:, None] // C == np.arange(2)[None, :]).astype(np.float32)
    arr["x"] = n(x)
    w, b = n(L0_tok_qkv_w), n(L0_tok_qkv_b)
    order = np.concatenate([np.arange(C) + C, np.arange(C)])
    arr["w_qk"] = _with_bias(w[order].T, b[order])
    arr["w_qk_swap"] = _with_bias(w[order ^ 1].T, b[order ^ 1])
    arr["w_v1"] = _with_bias(w[2 * C:].T, b[2 * C:])
    arr["w_p1"] = _with_bias(n(L0_tok_proj_w).T, n(L0_tok_proj_b))
    w = n(L0_attn_W_qkv)
    arr["w_q2"], arr["w_k2"], arr["w_v2"] = w[:C].T, w[C:2 * C].T, w[2 * C:].T
    arr["w_p2"] = _with_bias(n(L0_attn_W_proj).T, n(L0_attn_b_proj))
    arr["temp"] = n(L0_attn_temperature).reshape(1, 1)
    arr["w_i"] = _with_bias(n(L0_ffn_Wi).T, n(L0_ffn_bi))
    wr, br, ws, bs = n(L0_ffn_Wr), n(L0_ffn_br), n(L0_ffn_Ws), n(L0_ffn_bs)
    arr["experts"] = np.concatenate([wr.transpose(3, 0, 1, 2), br.transpose(2, 0, 1)[..., None]], 3)
    arr["shared"] = np.concatenate([ws[:, 0].transpose(2, 0, 1), bs[:, 0].T[..., None]], 2)
    arr["w_o"], arr["b_o"] = n(L0_ffn_Wo).T, n(L0_ffn_bo).reshape(1, C)
    arr["route"] = n(L0_ffn_route_id).reshape(1, -1)
    w, b = n(L1_attn_Wqkv), n(L1_attn_bqkv)
    arr["w_q3"], arr["w_k3"] = _with_bias(w[:, :C], b[:C]), _with_bias(w[:, C:2 * C], b[C:2 * C])
    arr["w_kv3"] = _with_bias(w[:, C:], b[C:])
    g = _with_bias(n(L1_ffn_proj_w).T, n(L1_ffn_proj_b))
    arr["w_gate"] = np.concatenate([g, g, g], 1)
    arr["w_bin"] = n(L1_ffn_weight)[0].reshape(NG, C, C // 2, 2).transpose(0, 2, 3, 1).reshape(P, -1)
    arr["scale"] = n(L1_ffn_scale).reshape(1, C)

    nc = _bacc.Bacc("TRN2", target_bir_lowering=False, num_devices=1)
    arrays, aps = {}, {}
    for k in ("w_qk", "w_qk_swap", "w_v1", "w_p1", "w_q2", "w_k2", "w_v2", "w_p2", "w_i", "b_o", "w_q3", "w_k3", "w_kv3", "w_gate"):
        arr[k] = np.pad(arr[k], ((0, P - arr[k].shape[0]), (0, 0)))
    for k, v in arr.items():
        v = np.ascontiguousarray(v)
        arrays["in_" + k] = v
        aps[k] = nc.dram_tensor("in_" + k, v.shape, mybir.dt.from_np(v.dtype), kind="ExternalInput").ap()
    o = nc.dram_tensor("out_0", (B, H * W, C), F32, kind="ExternalOutput").ap()
    build(nc, aps, o)
    return _run(nc, [arrays], core_ids=[0]).results[0]["out_0"]
```
